# Optimizing a Trainium2 kernel written in Bass

```python
import numpy as np
import jax
import jax.numpy as jnp

def _softmax(x, axis=-1):
    return jax.nn.softmax(x, axis=axis)

def _gelu(x):
    return jax.nn.gelu(x, approximate=True)

def _silu(x):
    return jax.nn.silu(x)

def _sigmoid(x):
    return jax.nn.sigmoid(x)

def _layernorm(x, axis=-1, eps=1e-05):
    m = jnp.mean(x, axis=axis, keepdims=True)
    v = jnp.var(x, axis=axis, keepdims=True)
    return (x - m) / jnp.sqrt(v + eps)

def _scatter_add(tgt, idx, src, axis=0):
    return tgt.at[idx].add(src)

def _segment_sum(src, seg, n):
    return jax.ops.segment_sum(src, seg, n)
kernel_name = 'mk_adj_preln_d4_adj_r2_f03cf6'

def setup_inputs(seed: int=0):
    np.random.seed(seed)
    _w = jnp.asarray

    def _rec_inputs():
        import jax
        import jax.numpy as jnp
        _gk = jax.random.key(seed)
        x = -0.0005207 + 1.001 * jax.random.normal(jax.random.fold_in(_gk, 1), (4096, 128), jnp.float32)
        _a = jax.random.bernoulli(jax.random.fold_in(_gk, 2), 0.000488281, (4096, 4096))
        _a = jnp.logical_or(_a, jnp.eye(4096, dtype=bool))
        _af = _a.astype(jnp.float32)
        _af = _af * jax.random.uniform(jax.random.fold_in(_gk, 3), (4096, 4096), jnp.float32, 0.05, 1)
        adj = _af
        return (x, adj)
    x, adj = _rec_inputs()

    def _L0_gnn_setup():
        import jax, jax.numpy as jnp
        import numpy as np
        key = jax.random.key(seed)
        k1, k2, k3, k4 = jax.random.split(key, 4)
        N, F_in, F_out = (4096, 128, 128)
        x = jax.random.normal(k1, (N, F_in), dtype=jnp.float32)
        adj = jax.random.uniform(k2, (N, N), dtype=jnp.float32)
        lim = 1.0 / np.sqrt(F_in)
        W = jax.random.uniform(k3, (F_out, F_in), dtype=jnp.float32, minval=-lim, maxval=lim)
        b = jax.random.uniform(k4, (F_out,), dtype=jnp.float32, minval=-lim, maxval=lim)
        return {'x': x, 'adj': adj, 'W': W, 'b': b}
    _L0_gnn_all = _L0_gnn_setup()
    _L0_gnn_in = {k: v for k, v in _L0_gnn_all.items() if k in ('W', 'b')}
    del _L0_gnn_all

    def _L1_gnn_setup():
        import jax, jax.numpy as jnp
        import numpy as np
        N = 4096
        IN = 128
        OUT = 128
        EDGE_P = 0.004
        key = jax.random.key(seed)
        k1, k2, k3, k4 = jax.random.split(key, 4)
        node_feats = jax.random.normal(k1, (N, IN), dtype=jnp.float32)
        a = (jax.random.uniform(k2, (N, N)) < EDGE_P).astype(jnp.float32)
        adj_matrix = jnp.maximum(a, a.T)
        W = jax.random.normal(k3, (OUT, IN), dtype=jnp.float32) / np.float32(np.sqrt(IN))
        b = jax.random.normal(k4, (OUT,), dtype=jnp.float32) * 0.01
        return {'node_feats': node_feats, 'adj_matrix': adj_matrix, 'W': W, 'b': b}
    _L1_gnn_all = _L1_gnn_setup()
    _L1_gnn_in = {k: v for k, v in _L1_gnn_all.items() if k in ('W', 'b')}
    del _L1_gnn_all

    def _L2_gnn_setup():
        import jax, jax.numpy as jnp
        import numpy as np
        N = 4096
        DIN = 128
        DOUT = 128
        EDGE_P = 0.004
        key = jax.random.key(seed)
        k1, k2, k3, k4, k5 = jax.random.split(key, 5)
        h = jax.random.normal(k1, (N, DIN), dtype=jnp.float32)
        adj = (jax.random.uniform(k2, (N, N)) < EDGE_P).astype(jnp.float32)
        xav_w = float(np.sqrt(6.0 / (DIN + DOUT)))
        weight = jax.random.uniform(k3, (DIN, DOUT), minval=-xav_w, maxval=xav_w, dtype=jnp.float32)
        xav_a = float(np.sqrt(6.0 / (DOUT + 1)))
        a_l = jax.random.uniform(k4, (DOUT,), minval=-xav_a, maxval=xav_a, dtype=jnp.float32)
        a_r = jax.random.uniform(k5, (DOUT,), minval=-xav_a, maxval=xav_a, dtype=jnp.float32)
        b = jnp.zeros((DOUT,), dtype=jnp.float32)
        return {'h': h, 'adj': adj, 'weight': weight, 'a_l': a_l, 'a_r': a_r, 'b': b}
    _L2_gnn_all = _L2_gnn_setup()
    _L2_gnn_in = {k: v for k, v in _L2_gnn_all.items() if k in ('weight', 'a_l', 'a_r', 'b')}
    del _L2_gnn_all

    def _L3_gnn_setup():
        import jax, jax.numpy as jnp
        import numpy as np
        N, H, HEADS = (2048, 128, 3)
        ALPHA = 0.2
        NEG_INF = -9000000000000000.0

        def _sign_adj(key, n, density):
            k1, k2 = jax.random.split(key)
            mask = jax.random.uniform(k1, (n, n)) < density
            sign = jnp.where(jax.random.uniform(k2, (n, n)) < 0.5, -1.0, 1.0)
            adj = jnp.where(mask, sign, 0.0).astype(jnp.float32)
            idx = jnp.arange(n)
            return adj.at[idx, idx].set(1.0)

        def _gru_cell(x, hstate, Wih, Whh, bih, bhh):
            gi = x @ Wih.T + bih
            gh = hstate @ Whh.T + bhh
            ir, iz, inn = jnp.split(gi, 3, axis=1)
            hr, hz, hn = jnp.split(gh, 3, axis=1)
            r = jax.nn.sigmoid(ir + hr)
            z = jax.nn.sigmoid(iz + hz)
            n = jnp.tanh(inn + r * hn)
            return (1.0 - z) * n + z * hstate

        def _gat_head(h, node_adj, edge_adj, W, a):
            hW = h @ W
            hp = (node_adj > 0).astype(hW.dtype) @ hW
            hm = (node_adj < 0).astype(hW.dtype) @ hW
            e_plus = jax.nn.leaky_relu(jnp.concatenate([hp, hm], axis=1) @ a, ALPHA)[:, 0]
            e_minus = jax.nn.leaky_relu(jnp.concatenate([hm, hp], axis=1) @ a, ALPHA)[:, 0]
            att = jnp.where(edge_adj > 0, e_plus[None, :], NEG_INF)
            att = jnp.where(edge_adj < 0, e_minus[None, :], att)
            att = jax.nn.softmax(att, axis=1)
            return att * edge_adj @ hW
        key = jax.random.key(seed)
        ks = jax.random.split(key, 16)
        std = 0.01
        gain = 1.414
        return {'h': jax.random.normal(ks[0], (N, H), jnp.float32), 'node_adj': _sign_adj(ks[1], N, 0.005), 'edge_adj': _sign_adj(ks[2], N, 0.005), 'gat_W': jax.random.normal(ks[3], (HEADS, H, H), jnp.float32) * (gain / np.sqrt(H, dtype=np.float32)), 'gat_a': jax.random.normal(ks[4], (HEADS, 2 * H, 1), jnp.float32) * 0.1, 'edge_Wih': jax.random.normal(ks[5], (3 * H, H), jnp.float32) * std, 'edge_Whh': jax.random.normal(ks[6], (3 * H, H), jnp.float32) * std, 'edge_bih': jnp.zeros((3 * H,), jnp.float32), 'edge_bhh': jnp.zeros((3 * H,), jnp.float32), 'node_Wih': jax.random.normal(ks[7], (3 * H, H), jnp.float32) * std, 'node_Whh': jax.random.normal(ks[8], (3 * H, H), jnp.float32) * std, 'node_bih': jnp.zeros((3 * H,), jnp.float32), 'node_bhh': jnp.zeros((3 * H,), jnp.float32)}
    _L3_gnn_all = _L3_gnn_setup()
    _L3_gnn_in = {k: v for k, v in _L3_gnn_all.items() if k in ('gat_W', 'gat_a', 'edge_Wih', 'edge_Whh', 'edge_bih', 'edge_bhh', 'node_Wih', 'node_Whh', 'node_bih', 'node_bhh')}
    del _L3_gnn_all
    return {'x': x, 'adj': adj, 'L0_gnn_W': _L0_gnn_in['W'], 'L0_gnn_b': _L0_gnn_in['b'], 'L1_gnn_W': _L1_gnn_in['W'], 'L1_gnn_b': _L1_gnn_in['b'], 'L2_gnn_weight': _L2_gnn_in['weight'], 'L2_gnn_a_l': _L2_gnn_in['a_l'], 'L2_gnn_a_r': _L2_gnn_in['a_r'], 'L2_gnn_b': _L2_gnn_in['b'], 'L3_gnn_gat_W': _L3_gnn_in['gat_W'], 'L3_gnn_gat_a': _L3_gnn_in['gat_a'], 'L3_gnn_edge_Wih': _L3_gnn_in['edge_Wih'], 'L3_gnn_edge_Whh': _L3_gnn_in['edge_Whh'], 'L3_gnn_edge_bih': _L3_gnn_in['edge_bih'], 'L3_gnn_edge_bhh': _L3_gnn_in['edge_bhh'], 'L3_gnn_node_Wih': _L3_gnn_in['node_Wih'], 'L3_gnn_node_Whh': _L3_gnn_in['node_Whh'], 'L3_gnn_node_bih': _L3_gnn_in['node_bih'], 'L3_gnn_node_bhh': _L3_gnn_in['node_bhh']}

def reference(x, adj, L0_gnn_W, L0_gnn_b, L1_gnn_W, L1_gnn_b, L2_gnn_weight, L2_gnn_a_l, L2_gnn_a_r, L2_gnn_b, L3_gnn_gat_W, L3_gnn_gat_a, L3_gnn_edge_Wih, L3_gnn_edge_Whh, L3_gnn_edge_bih, L3_gnn_edge_bhh, L3_gnn_node_Wih, L3_gnn_node_Whh, L3_gnn_node_bih, L3_gnn_node_bhh):
    import jax
    import jax.numpy as jnp

    def _L0_gnn_ref(x, adj, W, b):
        import jax, jax.numpy as jnp
        import numpy as np
        N = adj.shape[0]
        adj = adj + jnp.eye(N, dtype=adj.dtype)
        deg = adj.sum(axis=1)
        deg_inv_sqrt = deg ** (-0.5)
        deg_inv_sqrt = jnp.where(jnp.isinf(deg_inv_sqrt), 0.0, deg_inv_sqrt)
        adj_normalized = deg_inv_sqrt[:, None] * adj * deg_inv_sqrt[None, :]
        support = x @ W.T + b
        return adj_normalized @ support

    def _L1_gnn_ref(node_feats, adj_matrix, W, b):
        import jax, jax.numpy as jnp
        import numpy as np
        N = 4096
        IN = 128
        OUT = 128
        EDGE_P = 0.004
        n = adj_matrix.shape[0]
        adj = adj_matrix + jnp.eye(n, dtype=adj_matrix.dtype)
        deg = jnp.sum(adj, axis=1)
        dinv = jnp.where(deg > 0, deg ** (-0.5), 0.0)
        adj_norm = dinv[:, None] * adj * dinv[None, :]
        x = node_feats @ W.T + b
        mean = jnp.mean(x, axis=0, keepdims=True)
        std = jnp.std(x, axis=0, ddof=1, keepdims=True)
        x = (x - mean) / (std + 1e-06)
        return adj_norm @ x

    def _L2_gnn_ref(h, adj, weight, a_l, a_r, b):
        import jax, jax.numpy as jnp
        import numpy as np
        N = 4096
        DIN = 128
        DOUT = 128
        EDGE_P = 0.004
        x = h @ weight
        el = x @ a_l
        er = x @ a_r
        mask = adj != 0
        scores = el[:, None] + er[None, :]
        attn = jnp.exp(jax.nn.leaky_relu(scores, negative_slope=0.2))
        attn = jnp.where(mask, attn, 0.0)
        denom = jnp.maximum(attn.sum(axis=-1, keepdims=True), 1e-12)
        A = attn / denom
        out = A @ x + b
        return out

    def _L3_gnn_ref(h, node_adj, edge_adj, gat_W, gat_a, edge_Wih, edge_Whh, edge_bih, edge_bhh, node_Wih, node_Whh, node_bih, node_bhh):
        import jax, jax.numpy as jnp
        import numpy as np
        N, H, HEADS = (2048, 128, 3)
        ALPHA = 0.2
        NEG_INF = -9000000000000000.0

        def _sign_adj(key, n, density):
            k1, k2 = jax.random.split(key)
            mask = jax.random.uniform(k1, (n, n)) < density
            sign = jnp.where(jax.random.uniform(k2, (n, n)) < 0.5, -1.0, 1.0)
            adj = jnp.where(mask, sign, 0.0).astype(jnp.float32)
            idx = jnp.arange(n)
            return adj.at[idx, idx].set(1.0)

        def _gru_cell(x, hstate, Wih, Whh, bih, bhh):
            gi = x @ Wih.T + bih
            gh = hstate @ Whh.T + bhh
            ir, iz, inn = jnp.split(gi, 3, axis=1)
            hr, hz, hn = jnp.split(gh, 3, axis=1)
            r = jax.nn.sigmoid(ir + hr)
            z = jax.nn.sigmoid(iz + hz)
            n = jnp.tanh(inn + r * hn)
            return (1.0 - z) * n + z * hstate

        def _gat_head(h, node_adj, edge_adj, W, a):
            hW = h @ W
            hp = (node_adj > 0).astype(hW.dtype) @ hW
            hm = (node_adj < 0).astype(hW.dtype) @ hW
            e_plus = jax.nn.leaky_relu(jnp.concatenate([hp, hm], axis=1) @ a, ALPHA)[:, 0]
            e_minus = jax.nn.leaky_relu(jnp.concatenate([hm, hp], axis=1) @ a, ALPHA)[:, 0]
            att = jnp.where(edge_adj > 0, e_plus[None, :], NEG_INF)
            att = jnp.where(edge_adj < 0, e_minus[None, :], att)
            att = jax.nn.softmax(att, axis=1)
            return att * edge_adj @ hW
        dn = jnp.diag(node_adj)
        de = jnp.diag(edge_adj)
        idx = jnp.arange(node_adj.shape[0])
        node_adj_norm = node_adj.at[idx, idx].add(-dn)
        edge_adj_norm = edge_adj.at[idx, idx].add(-de)
        node_support = node_adj_norm @ h
        edge_output = _gru_cell(node_support, h, edge_Wih, edge_Whh, edge_bih, edge_bhh)
        edge_support = _gat_head(h, node_adj_norm, edge_adj_norm, gat_W[0], gat_a[0])
        for i in range(1, HEADS):
            edge_support = edge_support + _gat_head(h, node_adj_norm, edge_adj_norm, gat_W[i], gat_a[i])
        edge_support = edge_support / HEADS
        node_output = _gru_cell(edge_support, h, node_Wih, node_Whh, node_bih, node_bhh)
        return de[:, None] * edge_output + dn[:, None] * node_output
    h = jnp.maximum(_layernorm(x, axis=-1), 0.0)
    x = x + _L0_gnn_ref(h, adj, L0_gnn_W, L0_gnn_b)
    h = jnp.maximum(_layernorm(x, axis=-1), 0.0)
    x = x + _L1_gnn_ref(h, adj, L1_gnn_W, L1_gnn_b)
    h = jnp.maximum(_layernorm(x, axis=-1), 0.0)
    x = x + _L2_gnn_ref(h, adj, L2_gnn_weight, L2_gnn_a_l, L2_gnn_a_r, L2_gnn_b)
    h = jnp.maximum(_layernorm(x, axis=-1), 0.0)
    x = x + _L3_gnn_ref(h, adj, adj, L3_gnn_gat_W, L3_gnn_gat_a, L3_gnn_edge_Wih, L3_gnn_edge_Whh, L3_gnn_edge_bih, L3_gnn_edge_bhh, L3_gnn_node_Wih, L3_gnn_node_Whh, L3_gnn_node_bih, L3_gnn_node_bhh)
    return x

_drawn_inputs = setup_inputs


def setup_inputs(seed=0):
    import zlib

    import numpy as np

    out = dict(_drawn_inputs(seed))
    spreads = {'L2_gnn_b': (0.0, 0.1),
     'L3_gnn_edge_bih': (0.0, 0.558),
     'L3_gnn_edge_bhh': (0.0, 0.8),
     'L3_gnn_node_bih': (0.0, 0.513),
     'L3_gnn_node_bhh': (0.0, 0.8)}
    factors = {'L1_gnn_b': 8.0,
     'L3_gnn_gat_W': 8.0,
     'L3_gnn_gat_a': 8.0,
     'L3_gnn_edge_Wih': 4.375,
     'L3_gnn_edge_Whh': 7.627,
     'L3_gnn_node_Wih': 8.0,
     'L3_gnn_node_Whh': 7.821}
    for name, (base, spread) in spreads.items():
        noise = np.random.default_rng([zlib.crc32(name.encode()), seed]).standard_normal(out[name].shape)
        drawn = base * np.exp(spread * noise) if base else spread * noise
        out[name] = jnp.asarray(drawn.astype(out[name].dtype))
    for name, factor in factors.items():
        out[name] = (out[name] * factor).astype(out[name].dtype)
    return out
```

```python
from contextlib import ExitStack

import concourse.bass as bass
from concourse import mybir
from concourse.alu_op_type import AluOpType as ALU

ACT = mybir.ActivationFunctionType
AX = mybir.AxisListType
F32 = mybir.dt.float32
F32R = mybir.dt.float32r
BF16 = mybir.dt.bfloat16
I32 = mybir.dt.int32

P = 128
N = 4096
T = N // P
W = 512
C = N // W
Q = W // P
G = T // Q
UNIT = Q * W
HEADS = 3
EPS = 1e-5
SLOPE = 0.2
LN2 = 0.6931471805599453

WINDOWS = P // (3 * HEADS)
STEP = 120.0
LIFT = 78.0
VCOLS = 3 * HEADS * WINDOWS
ECOLS = 3 * 2 * HEADS + 1
SCORES = 2 * HEADS
RING_OUT = 4
BUFS = 12
GBUFS = 8
WINDOW_MIN = 2.3e-19
ROUND = 12582912.0

LN_STEPS = {"deg": 5, "agg0": 8, "agg1": 8, "gat": 13}
LN_ROOT = {"deg": 3, "agg0": 6, "agg1": 6, "gat": 9}
U_STEPS = 7
EDGE_STEPS = 4
NORM_STEPS, NORM_EXP = 17, 14
PREP_HEAD, PREP_SIGN = 9, 8
CELL_A, CELL_B = 3, 6
CELL_STEPS = 2 * CELL_B + 1


def at(c, step, off, size):
    if isinstance(c, int):
        return slice(step * c + off, step * c + off + size)
    return bass.ds(c * step + off, size)


class Steps:

    def __init__(self, eng, sem, k, c):
        self.eng, self.sem, self.k, self.base, self.n = eng, sem, k, c * k, 0

    def inc(self, instruction):
        self.n += 1
        instruction.then_inc(self.sem, 1)

    def link(self, instruction):
        self.inc(instruction)
        self.eng.wait_ge(self.sem, self.base + self.n)

    def done(self):
        assert self.n == self.k, (self.sem, self.n)


def over_chunks(eng, body):
    body(0, True)
    with eng.Fori(1, C) as c:
        body(c, False)


def build(nc, x_d, rows_d, cols_d, diag_d, w_d, gru_d, col_d, row_d, out_d):
    with ExitStack() as ctx:
        def sb(name, shape, dt=F32):
            return ctx.enter_context(nc.sbuf_tensor(name, shape, dt))

        def sem(name):
            return ctx.enter_context(nc.semaphore(name))

        def shared(name, shape, dt):
            with nc.sbuf_tensor(name, shape, dt) as view:
                return view

        bank = [ctx.enter_context(nc.psum_tensor(f"bank{i}", [P, W], F32)) for i in range(8)]

        a_lo = shared("a_lo", [P, G * UNIT], F32R)
        ring = sb("ring", [P, G * UNIT])
        x = sb("x", [P, N])
        s_hi = shared("s_hi", [P, N], F32R)
        reg1 = sb("reg1", [P, N])
        s_lo = shared("s_lo", [P, N], F32R)
        reg2 = sb("reg2", [P, N])
        reg3 = sb("reg3", [P, N])
        reg4 = sb("reg4", [P, N + W])
        a_hi = shared("a_hi", [P, 8192], F32R)
        work = sb("work", [P, 8192])
        half = sb("half", [P, W])
        outT = sb("outT", [P, W])
        hn = sb("hn", [P, W])
        hT = sb("hT", [P, W])
        wts = sb("wts", [P, 10 * P])
        gru = sb("gru", [P, 4 * 3 * P])
        cols = sb("cols", [P, 21])
        diag = sb("diag", [P, T])
        ident = sb("ident", [P, P])
        ones = sb("ones", [P, P])
        offdiag = sb("offdiag", [P, P])
        pick = sb("pick", [SCORES, SCORES * P])
        b2all = sb("b2all", [P, P])
        wel = sb("wel", [P, P])
        wlr = sb("wlr", [P, 2])
        wa = sb("wa", [P, SCORES])
        gb = sb("gb", [P, 8])
        dinv0 = sb("dinv0", [P, T])
        dinv1 = sb("dinv1", [P, T])
        stats = sb("stats", [P, Q * 6])
        mv = sb("mv", [P, Q * 2])
        rstd = sb("rstd", [P, 3 * Q])
        bnst = sb("bnst", [P, C * 6])
        bnmv = sb("bnmv", [P, 6])
        elr = sb("elr", [P, 2 * T])
        el02 = sb("el02", [P, T])
        er02 = sb("er02", [P, T])
        den = sb("den", [P, 4 * Q])
        esum = sb("esum", [P, Q * SCORES])
        e6 = sb("e6", [P, T * SCORES])
        neg_e = sb("neg_e", [P, T * HEADS])
        d_e = sb("d_e", [P, T * HEADS])
        cnt = sb("cnt", [P, T])
        top = sb("top", [P, 20])
        flag = sb("flag", [1, 1], I32)
        c0 = sb("c0", [P, 3 * HEADS])
        wconst = sb("wconst", [P, 2 * WINDOWS])
        shift = sb("shift", [P, HEADS * WINDOWS])
        gd = sb("gd", [P, 7 * Q * HEADS])
        nr = sb("nr", [P, Q * SCORES])

        w0t, w1t, w2, w2t = (wts[:, i * P:(i + 1) * P] for i in range(4))
        gat_w = [wts[:, (4 + k) * P:(5 + k) * P] for k in range(HEADS)]
        gat_wt = [wts[:, (7 + k) * P:(8 + k) * P] for k in range(HEADS)]

        def gate_w(cell, hidden, gate):
            i = (2 * cell + hidden) * 3 + gate
            return gru[:, i * P:(i + 1) * P]

        rows = reg4[0:1, 0:2 * P]
        degp = reg4[:, 512:512 + 2 * T]
        deg = reg4[:, 1024:1024 + 7 * T]
        gmask = work[:, 0:UNIT].bitcast(BF16)
        gtile = work[:, 2048:2048 + GBUFS * W]
        den_v, den_p = work[:, 6144:6144 + W], work[:, 6656:6656 + W]
        SP, ER = 7168, 7168 + T * ECOLS
        sp_all = work[:, SP:SP + T * ECOLS // 2].bitcast(BF16)
        sm_all = work[:, SP + T * ECOLS // 2:ER].bitcast(BF16)
        eraw = work[:, ER:ER + Q * ECOLS]
        ucut = work[:, ER + Q * ECOLS:ER + Q * ECOLS + 2 * Q * SCORES]
        pmask = work[:, 0:UNIT].bitcast(BF16)
        mmask = work[:, UNIT:2 * UNIT].bitcast(BF16)
        vcut = work[:, 4096:4096 + Q * VCOLS]
        VB = Q * HEADS * WINDOWS
        dsum, dok, dwin, dsel = (work[:, 4608 + i * VB:4608 + (i + 1) * VB] for i in range(4))
        VT = T * HEADS * WINDOWS
        vtmp = [work[:, i * VT:(i + 1) * VT] for i in range(3)]
        tile = work[:, 0:BUFS * W]
        negg = work[:, BUFS * W:(BUFS + HEADS) * W]
        vp = reg3[:, 0:T * VCOLS // 2].bitcast(BF16)
        vm = reg3[:, N // 2:N // 2 + T * VCOLS // 2].bitcast(BF16)
        grows = reg4[0:SCORES, :]
        spare = ring[:, RING_OUT * UNIT:G * UNIT]
        rden = spare[:, 0:HEADS * W]
        nk = spare[:, 3 * W:6 * W]
        nsT, esT = spare[:, 6 * W:7 * W], spare[:, 7 * W:8 * W]
        gr, gz, gn, gt = (spare[:, (8 + i) * W:(9 + i) * W] for i in range(4))
        cell_out = spare[:, 12 * W:13 * W]
        cells = spare[:, 13 * W:14 * W]
        res = spare[:, 14 * W:15 * W]
        slow = spare[:, 15 * W:16 * W]
        nmask = reg3[:, 0:UNIT // 2].bitcast(BF16)

        s_passed = sem("waits_passed")
        s_const, s_xin = sem("constants_loaded"), sem("x_loaded")
        s_rows = [sem(f"row_tile_loaded{i}") for i in range(4)]
        s_unit = [sem(f"unit_loaded{i}") for i in range(G)]
        s_pc, s_dc, s_pw, s_dw = sem("pool_constants"), sem("dve_constants"), sem("weights_made"), sem("weights_kept")
        s_degd, s_dega, s_degs = sem("degree_half_dve"), sem("degree_half_act"), sem("degree_steps")
        s_degr = sem("degree_root")
        NODE = ("deg", "agg0", "agg1", "gat")
        s_ln, s_root, s_hturn, s_hT, s_proj, s_pkeep = (
            {p: sem(f"{p}_{what}") for p in NODE}
            for what in ("norm_steps", "norm_root", "h_turned", "hT_kept", "projected", "projection_kept"))
        s_pkeep_act = sem("agg1_projection_kept_act")
        s_scale = {p: sem(f"{p}_scale_steps") for p in ("agg0", "agg1")}
        s_bnstat = sem("bn_statistics")
        s_bn, s_bnroot, s_bnnorm, s_bnturn = sem("bn_steps"), sem("bn_root"), sem("bn_normalised"), sem("bn_turned")
        s_ahi, s_alo = ({p: sem(f"{p}_unit_{what}") for p in ("agg0", "agg1")} for what in ("high", "low"))
        PASSES = ("agg0", "agg1", "gat", "edge", "norm", "out")
        s_mm = {p: sem(f"{p}_unit_multiplied") for p in PASSES}
        s_half, s_sum, s_turn = ({p: sem(f"{p}_{what}") for p in PASSES[:5]}
                                 for what in ("half_kept", "sum_kept", "sum_turned"))
        s_cut = {p: sem(f"{p}_turned_kept") for p in ("edge", "norm")}
        s_mask = {p: sem(f"{p}_masks") for p in ("gat", "edge", "norm")}
        s_e02, s_hall = sem("gat_exponentials"), sem("gat_hT_stored")
        s_gexp, s_gy, s_gmm = sem("gat_exp"), sem("gat_weights"), sem("gat_tile_multiplied")
        s_gdd, s_gdp, s_gden = sem("gat_den_dve"), sem("gat_den_pool"), sem("gat_den_summed")
        s_fix = {p: sem(f"{p}_diagonal_cleared") for p in ("edge", "norm", "out")}
        s_ee, s_prep, s_ptop, s_vexp = sem("edge_steps"), sem("prep_steps"), sem("prep_top"), sem("prep_exp")
        s_flag = sem("flag_ready")
        s_ne, s_nexp, s_nturn, s_nrow = sem("norm_steps"), sem("norm_exp"), sem("norm_rows_turned"), sem("norm_rows_kept")
        s_clamp, s_exp, s_y, s_used = sem("out_clamped"), sem("out_exp"), sem("out_weights"), sem("out_tile_used")
        s_slow = sem("out_negative_steps")
        s_gg, s_ggk, s_rr, s_rrk = sem("guards_spread"), sem("guards_kept"), sem("dens_spread"), sem("dens_kept")
        s_nk, s_es, s_esk = sem("out_sums_kept"), sem("edge_support"), sem("edge_support_kept")
        s_gm, s_ga, s_gv = sem("gates_multiplied"), sem("gates_tanh"), sem("gates_steps")
        s_ot, s_res, s_store = sem("out_turned"), sem("out_result"), sem("out_stored")

        def hold(eng):
            eng.sem_inc(s_passed, 1)

        def loaded(p, c, g):
            if p == "out":
                return s_unit[g % RING_OUT], c * 32 + (16 * C * 5 + 16 * (g // RING_OUT + 1))
            return s_unit[g], c * 16 + (16 * C * PASSES.index(p) + 16)

        def ring_at(p, g, off=0, size=UNIT):
            slot = g % RING_OUT if p == "out" else g
            return slice(slot * UNIT + off, slot * UNIT + off + size)

        last_reader = {"agg0": s_mm["agg0"], "agg1": s_mm["agg1"], "gat": s_mask["gat"],
                       "edge": s_mask["edge"], "norm": s_mask["norm"], "out": s_mm["out"]}

        block = ctx.enter_context(nc.Block())

        @block.sync
        def _(sp):
            sp.dma_start(x[:, :].rearrange("p (t f) -> p t f", f=P),
                         x_d.rearrange("(t p) f -> p t f", p=P)).then_inc(s_xin, 16)
            for dst, src in ((wts, w_d), (cols, col_d), (rows, row_d), (gru, gru_d), (diag, diag_d)):
                sp.dma_start(dst[:, :], src).then_inc(s_const, 16)

            for s in range(4):
                sp.dma_start(ring[:, s * N:(s + 1) * N], rows_d[s * P:(s + 1) * P, :]).then_inc(s_rows[s], 16)
            with sp.Fori(1, C) as c:
                for s in range(4):
                    sp.wait_ge(s_degd, c * 4 + (s - 3))
                    sp.wait_ge(s_dega, c * 4 + (s - 3))
                    sp.dma_start(ring[:, s * N:(s + 1) * N], rows_d[at(c, W, s * P, P), :]).then_inc(s_rows[s], 16)

            def load(p, c, g):
                sp.dma_start(ring[:, ring_at(p, g)], cols_d[at(c, G * P, g * P, P), :]).then_inc(loaded(p, 0, g)[0], 16)

            before = None
            for p in PASSES:
                slots = RING_OUT if p == "out" else G
                for g in range(G):
                    if g >= slots:
                        sp.wait_ge(last_reader[p], g - slots + 1)
                    elif before is None:
                        sp.wait_ge(s_degd, T - 3 + g // 2)
                        sp.wait_ge(s_dega, T - 3 + g // 2)
                    else:
                        sp.wait_ge(last_reader[before], G * (C - 1) + g + 1)
                    load(p, 0, g)
                with sp.Fori(1, C) as c:
                    for g in range(G):
                        sp.wait_ge(last_reader[p], c * G + (g - slots + 1))
                        load(p, c, g)
                before = p

        @block.gpsimd
        def _(pool):
            pool.memset(ident[:, :], 0.0).then_inc(s_pc, 1)
            pool.memset(ones[:, :], 1.0).then_inc(s_pc, 1)
            pool.memset(grows[:, N:N + W], 0.0).then_inc(s_pc, 1)
            pool.wait_ge(s_pc, 3)
            pool.affine_select(out=ident[:, :], in_=ident[:, :], compare_op=ALU.not_equal, fill=1.0,
                               base=0, pattern=[[-1, P]], channel_multiplier=1).then_inc(s_pc, 1)

            def gat_body(c, first):
                if not first:
                    pool.wait_ge(s_gden, c)
                for g in range(G):
                    for q in range(1, Q):
                        m = g * Q + q
                        y = gtile[:, (m % GBUFS) * W:(m % GBUFS + 1) * W]
                        pool.wait_ge(s_gy, c * T + (m + 1))
                        if m == 1:
                            hold(pool)
                            pool.tensor_copy(den_p, y).then_inc(s_gdp, 1)
                        else:
                            pool.wait_ge(s_gdp, c * (T - G) + (g * (Q - 1) + q - 1))
                            pool.tensor_tensor(den_p, den_p, y, ALU.add).then_inc(s_gdp, 1)
            over_chunks(pool, gat_body)

            pool.wait_ge(s_flag, 1)
            negative = pool.value_load(flag[0:1, 0:1], min_val=0, max_val=1)

            def out_body(c, first):
                pool.wait_ge(s_ggk, c + 1)
                for m in range(T * HEADS):
                    t, k = m // HEADS, m % HEADS
                    if m >= BUFS or not first:
                        pool.wait_ge(s_used, c * (T * HEADS) + (m + 1 - BUFS))
                        hold(pool)
                    pool.tensor_scalar(tile[:, (m % BUFS) * W:(m % BUFS + 1) * W], negg[:, k * W:(k + 1) * W],
                                       neg_e[:, t * HEADS + k:t * HEADS + k + 1], -3.0e38,
                                       ALU.min, ALU.max).then_inc(s_clamp, 1)
            with pool.If(negative == 0):
                over_chunks(pool, out_body)

        @block.scalar
        def _(act):
            def root(p, c):
                act.wait_ge(s_ln[p], c * LN_STEPS[p] + LN_ROOT[p])
                act.activation(rstd[:, Q:2 * Q], rstd[:, 0:Q], ACT.Sqrt).then_inc(s_root[p], 1)

            def keep_hT(p, c, first, func):
                act.wait_ge(s_hturn[p], c + 1)
                if not first:
                    act.wait_ge(s_proj[p], c)
                elif p != "deg":
                    act.wait_ge(s_proj[NODE[NODE.index(p) - 1]], C)
                act.activation(hT[:, :], bank[3][:, :], func).then_inc(s_hT[p], 1)

            def keep_half(p, c, first, m=P):
                if p == "gat":
                    act.wait_ge(s_gmm, c * T + T // 2)
                else:
                    act.wait_ge(s_mm[p], c * G + G // 2)
                if not first:
                    act.wait_ge(s_sum[p], c)
                elif p != "agg0":
                    act.wait_ge(s_sum[PASSES[PASSES.index(p) - 1]], C)
                act.activation(half[0:m, :], bank[0][0:m, :], ACT.Copy).then_inc(s_half[p], 1)

            def deg_body(c, first):
                for s in range(4):
                    act.wait_ge(s_rows[s], c * 16 + 16)
                    if s or not first:
                        act.wait_ge(s_dega, c * 4 + s)
                    act.activation(work[:, 0:N // 2], ring[:, s * N + N // 2:(s + 1) * N], ACT.Copy,
                                   accum_out=degp[:, at(c, 2 * Q, 2 * s + 1, 1)]).then_inc(s_dega, 1)
                    if s == 0:
                        root("deg", c)
                    if s == 2:
                        keep_hT("deg", c, first, ACT.Relu)
            over_chunks(act, deg_body)
            act.wait_ge(s_degs, 3)
            act.activation(deg[:, 3 * T:5 * T], deg[:, T:3 * T], ACT.Sqrt).then_inc(s_degr, 1)

            def project_keep(p, c, first):
                act.wait_ge(s_proj[p], c + 1)
                if p == "agg0":
                    act.activation(reg3[:, at(c, W, 0, W)], bank[4][:, :], ACT.Identity,
                                   bias=cols[:, 0:1]).then_inc(s_pkeep[p], 1)
                else:
                    act.activation(reg3[:, at(c, W, 0, W)], bank[4][:, :], ACT.Copy)
                    act.activation(reg4[:, at(c, W, 0, W)], bank[5][:, :], ACT.Copy).then_inc(s_pkeep_act, 1)

            for p in ("agg0", "agg1"):
                def agg_body(c, first, p=p):
                    for g in range(G):
                        if not first and g == 3:
                            root(p, c - 1)
                        if not first and g == 5:
                            finish_hT(p, c)
                        if not first and g == 7:
                            project_keep(p, c - 1, False)
                        act.wait_ge(*loaded(p, c, g))
                        if g >= 4 or not first:
                            act.wait_ge(s_mm[p], c * G + (g - 3))
                        elif p == "agg1":
                            act.wait_ge(s_mm["agg0"], G * C - 3 + g)
                        elif g == 0:
                            act.wait_ge(s_dega, T)
                        act.activation(a_hi[:, (g % 4) * UNIT:(g % 4 + 1) * UNIT],
                                       ring[:, ring_at(p, g)], ACT.Copy).then_inc(s_ahi[p], 1)
                        if g == 7:
                            keep_half(p, c, first)

                def finish_hT(p, c):
                    act.wait_ge(s_hturn[p], c)
                    if p == "agg0":
                        act.wait_ge(s_proj["deg"], C)
                    else:
                        act.wait_ge(s_proj["agg0"], C)
                    act.wait_ge(s_proj[p], c - 1)
                    act.activation(hT[:, :], bank[3][:, :], ACT.Relu).then_inc(s_hT[p], 1)

                over_chunks(act, agg_body)
                root(p, C - 1)
                finish_hT(p, C)
                project_keep(p, C - 1, False)
                if p == "agg0":
                    act.wait_ge(s_bn, 2)
                    act.activation(bnmv[:, 3:4], bnmv[:, 2:3], ACT.Sqrt).then_inc(s_bnroot, 1)

            act.wait_ge(s_pkeep["agg1"], C)
            elr_v = elr[:, :].rearrange("p (t h) -> p h t", h=2)
            act.activation(el02[:, :], elr_v[:, 0, :], ACT.Exp, scale=SLOPE).then_inc(s_e02, 1)
            act.activation(er02[:, :], elr_v[:, 1, :], ACT.Exp, scale=SLOPE).then_inc(s_e02, 1)
            act.wait_ge(s_pkeep_act, C)
            act.wait_ge(s_mm["agg1"], G * C)

            def store_hT(c):
                act.wait_ge(s_hturn["gat"], c)
                act.wait_ge(s_proj["agg1"], C)
                act.wait_ge(s_proj["gat"], c - 1)
                act.activation(hT[:, :], bank[3][:, :], ACT.Copy).then_inc(s_hT["gat"], 1)
                act.activation(reg2[:, at(c, W, -W, W)], bank[3][:, :], ACT.Copy).then_inc(s_hall, 1)

            def gat_body(c, first):
                for g in range(G):
                    if not first and g == 3:
                        root("gat", c - 1)
                    if not first and g == 5:
                        store_hT(c)
                    for q in range(Q):
                        m = g * Q + q
                        b = m % GBUFS
                        if g >= 2 or not first:
                            act.wait_ge(s_gmm, c * T + (m - GBUFS + 1))
                            if q == 0:
                                act.wait_ge(s_gdd, c * G + (g - 1))
                            else:
                                act.wait_ge(s_gdp, c * (T - G) + ((g - 2) * (Q - 1) + q))
                            hold(act)
                        act.activation(gtile[:, b * W:(b + 1) * W], reg4[:, at(c, W, 0, W)], ACT.Exp,
                                       bias=elr[:, 2 * m + 1:2 * m + 2], scale=1 - SLOPE).then_inc(s_gexp, 1)
                    if g == 5:
                        keep_half("gat", c, first)
            over_chunks(act, gat_body)
            root("gat", C - 1)
            store_hT(C)

            def cut(p, c):
                act.wait_ge(s_turn[p], c + 1)
                if p == "edge":
                    act.activation(eraw[:, :], bank[2][:, 0:Q * ECOLS], ACT.Copy).then_inc(s_cut[p], 1)
                else:
                    act.activation(vcut, bank[2][:, 0:Q * VCOLS], ACT.Copy).then_inc(s_cut[p], 1)

            def edge_body(c, first):
                if not first:
                    if not isinstance(c, int):
                        act.wait_ge(s_ee, c * EDGE_STEPS - EDGE_STEPS)
                    cut("edge", c - 1)
                keep_half("edge", c, first, ECOLS)
            over_chunks(act, edge_body)
            act.wait_ge(s_ee, (C - 1) * EDGE_STEPS)
            cut("edge", C - 1)

            for sign in range(2):
                act.wait_ge(s_prep, PREP_HEAD + sign * PREP_SIGN + 2)
                act.activation(vtmp[1], vtmp[1], ACT.Exp).then_inc(s_vexp, 1)

            def guards(c):
                act.wait_ge(s_ne, c * NORM_STEPS + NORM_EXP)
                act.activation(gd[:, 5 * Q * HEADS:6 * Q * HEADS], gd[:, 4 * Q * HEADS:5 * Q * HEADS],
                               ACT.Exp).then_inc(s_nexp, 1)

            def guard_rows(c):
                act.wait_ge(s_nturn, c + 1)
                act.activation(grows[:, at(c, W, 0, W)], bank[3][0:SCORES, :], ACT.Copy).then_inc(s_nrow, 1)

            def norm_body(c, first):
                if not first:
                    act.wait_ge(s_ne, c * NORM_STEPS - NORM_STEPS)
                    cut("norm", c - 1)
                    guards(c - 1)
                keep_half("norm", c, first, VCOLS)
                if not first:
                    guard_rows(c - 1)
            act.wait_ge(s_prep, PREP_HEAD + 2 * PREP_SIGN)
            over_chunks(act, norm_body)
            act.wait_ge(s_ne, (C - 1) * NORM_STEPS)
            cut("norm", C - 1)
            guards(C - 1)
            guard_rows(C - 1)

            SPREAD = (4, 6, 7)

            def keep_guards(c):
                act.wait_ge(s_gg, c + 1)
                act.wait_ge(s_clamp, c * (T * HEADS))
                for k in range(HEADS):
                    last = act.activation(negg[:, k * W:(k + 1) * W], bank[SPREAD[k]][:, :], ACT.Copy)
                last.then_inc(s_ggk, 1)

            def keep_dens(c, first):
                act.wait_ge(s_rr, c + 1)
                if not first:
                    act.wait_ge(s_nk, c)
                for k in range(HEADS):
                    last = act.activation(rden[:, k * W:(k + 1) * W], bank[5 + k][:, :], ACT.Copy)
                last.then_inc(s_rrk, 1)

            def keep_edge_support(c):
                act.wait_ge(s_es, c)
                act.wait_ge(s_gm, c * 2 - 2)
                act.activation(esT, bank[4][:, :], ACT.Copy, scale=1.0 / HEADS).then_inc(s_esk, 1)

            def gates(c, cell):
                act.wait_ge(s_gm, c * 2 + (cell - 1))
                act.wait_ge(s_gv, c * CELL_STEPS + (cell * CELL_B - CELL_STEPS))
                act.activation(gr, bank[5][:, :], ACT.Tanh, bias=gb[:, 4 * cell:4 * cell + 1], scale=0.5)
                act.activation(gz, bank[6][:, :], ACT.Tanh, bias=gb[:, 4 * cell + 1:4 * cell + 2],
                               scale=0.5).then_inc(s_ga, 1)

            def candidate(c, cell):
                act.wait_ge(s_gv, c * CELL_STEPS + (cell * CELL_B - CELL_STEPS + CELL_A))
                act.activation(gn, gt, ACT.Tanh).then_inc(s_ga, 1)

            def store(c):
                act.wait_ge(s_res, c)
                act.dma_start(out_d.rearrange("(t p) f -> p t f", p=P)[:, at(c, Q, -Q, Q), :],
                              res.rearrange("p (t f) -> p t f", f=P)).then_inc(s_store, 16)

            def out_body(c, first):
                for g in range(G):
                    if not first:
                        if g == 2:
                            gates(c, 0)
                        if g == 3:
                            candidate(c, 0)
                            keep_edge_support(c)
                        if g == 5:
                            gates(c, 1)
                        if g == 6:
                            candidate(c, 1)
                        if g == 7:
                            store(c)
                    if g == 3:
                        keep_dens(c, first)
                    for m in range(g * Q * HEADS, (g + 1) * Q * HEADS):
                        t, k, b = m // HEADS, m % HEADS, m % BUFS
                        act.wait_ge(s_clamp, c * (T * HEADS) + (m + 1))
                        act.activation(tile[:, b * W:(b + 1) * W], tile[:, b * W:(b + 1) * W], ACT.Exp,
                                       bias=e6[:, t * SCORES + k:t * SCORES + k + 1]).then_inc(s_exp, 1)
                keep_guards(c + 1)

            keep_guards(0)
            over_chunks(act, out_body)
            for cell in range(2):
                gates(C, cell)
                candidate(C, cell)
                if cell == 0:
                    keep_edge_support(C)
            store(C)
            act.wait_ge(s_store, 16 * C)

        @block.vector
        def _(dve):
            def spread(ap, n, axis=2):
                shape = [P, ap.shape[1]]
                shape.insert(axis, n)
                return ap.unsqueeze(axis).to_broadcast(shape)

            s = Steps(dve, s_dc, 2, 0)
            for b in range(WINDOWS):
                dve.memset(wconst[:, b:b + 1], STEP * b + LIFT)
                dve.memset(wconst[:, WINDOWS + b:WINDOWS + b + 1], float(WINDOWS - b))
            dve.wait_ge(s_pc, 4)
            dve.tensor_scalar(offdiag[:, :], ident[:, :], -1.0, 1.0, ALU.mult, ALU.add)
            s.inc(dve.tensor_copy(pick[:, :].rearrange("p (r m) -> p r m", r=SCORES),
                                  ident[0:SCORES, 0:SCORES].unsqueeze(2).to_broadcast([SCORES, SCORES, P])))
            dve.wait_ge(s_const, 16 * 5)
            for cell in range(2):
                bi, bh = 9 + 6 * cell, 12 + 6 * cell
                dve.tensor_tensor(gb[:, 4 * cell:4 * cell + 2], cols[:, bi:bi + 2], cols[:, bh:bh + 2], ALU.add)
                dve.tensor_copy(gb[:, 4 * cell + 2:4 * cell + 3], cols[:, bi + 2:bi + 3])
                last = dve.tensor_copy(gb[:, 4 * cell + 3:4 * cell + 4], cols[:, bh + 2:bh + 3])
            s.link(last)
            s.done()
            gb_v = gb[:, :].rearrange("p (c g) -> p c g", g=4)[:, :, 0:2]
            s = Steps(dve, s_dw, 2, 0)
            s.inc(dve.tensor_scalar(gb_v, gb_v, 0.5, None, ALU.mult))
            dve.wait_ge(s_pw, 1)
            dve.tensor_copy(wlr[:, :], bank[7][:, 0:2])
            dve.tensor_copy(wel[:, :], bank[7][:, 0:1].to_broadcast([P, P]))
            dve.tensor_copy(wa[:, :].rearrange("p (h k) -> p h k", h=2),
                            bank[7][:, 2:2 + SCORES].rearrange("p (k h) -> p h k", h=2))
            s.inc(dve.tensor_copy(b2all[:, :], bank[6][:, 0:P]))
            s.done()

            def per_tile(ap):
                return ap.rearrange("p (q f) -> p q f", q=Q)

            def norm_in(s, c):
                for q in range(Q):
                    last = dve.bn_stats(stats[:, q * 6:(q + 1) * 6], x[:, at(c, W, q * P, P)])
                s.link(last)
                hold(dve)
                for q in range(Q):
                    last = dve.bn_aggr(mv[:, q * 2:(q + 1) * 2], stats[:, q * 6:(q + 1) * 6])
                s.link(last)
                s.inc(dve.tensor_scalar(rstd[:, 0:Q], mv[:, 1:2 * Q:2], EPS, None, ALU.add))

            def norm_out(s, p, c, cc):
                dve.wait_ge(s_root[p], cc)
                s.link(dve.reciprocal(rstd[:, 2 * Q:3 * Q], rstd[:, Q:2 * Q]))
                for q in range(Q):
                    last = dve.tensor_scalar(hn[:, q * P:(q + 1) * P], x[:, at(c, W, q * P, P)],
                                             mv[:, 2 * q:2 * q + 1], rstd[:, 2 * Q + q:2 * Q + q + 1],
                                             ALU.subtract, ALU.mult)
                return last

            dve.wait_ge(s_xin, 16)

            def deg_body(c, first):
                s = Steps(dve, s_ln["deg"], LN_STEPS["deg"], c)
                for t in range(4):
                    if t == 0:
                        norm_in(s, c)
                    if t == 1:
                        if not first:
                            dve.wait_ge(s_hturn["deg"], c)
                        s.inc(norm_out(s, "deg", c, c + 1))
                        s.done()
                    dve.wait_ge(s_rows[t], c * 16 + 16)
                    dve.tensor_reduce(degp[:, at(c, 2 * Q, 2 * t, 1)], ring[:, t * N:t * N + N // 2],
                                      AX.X, ALU.add).then_inc(s_degd, 1)
                dve.wait_ge(s_proj["deg"], c + 1)
                dve.tensor_copy(reg3[:, at(c, W, 0, W)], bank[4][:, :]).then_inc(s_pkeep["deg"], 1)
            over_chunks(dve, deg_body)

            s = Steps(dve, s_degs, 5, 0)
            dve.wait_ge(s_degd, T)
            dve.wait_ge(s_dega, T)
            degp_v = degp[:, :].rearrange("p (t h) -> p h t", h=2)
            s.link(dve.tensor_tensor(deg[:, 0:T], degp_v[:, 0, :], degp_v[:, 1, :], ALU.add))
            s.link(dve.tensor_scalar(deg[:, 0:T], deg[:, 0:T], 1.0, None, ALU.add))
            dve.tensor_scalar(deg[:, 2 * T:3 * T], deg[:, 0:T], 1.0e-30, None, ALU.max)
            s.inc(dve.scalar_tensor_tensor(deg[:, T:2 * T], deg[:, 0:T], 0.0, deg[:, 0:T], ALU.is_equal, ALU.add))
            dve.wait_ge(s_degr, 1)
            s.link(dve.reciprocal(deg[:, 5 * T:7 * T], deg[:, 3 * T:5 * T]))
            dve.scalar_tensor_tensor(dinv0[:, :], deg[:, 0:T], 0.0, deg[:, 5 * T:6 * T], ALU.not_equal, ALU.mult)
            s.link(dve.scalar_tensor_tensor(dinv1[:, :], deg[:, 0:T], 0.0, deg[:, 6 * T:7 * T], ALU.is_gt, ALU.mult))
            s.done()

            def scale(p, g):
                s = Steps(dve, s_scale[p], 3, g)
                dinv = (dinv0 if p == "agg0" else dinv1)[:, g * Q:(g + 1) * Q]
                if p == "agg0":
                    src = reg3[:, g * W:(g + 1) * W]
                else:
                    dve.wait_ge(s_bnturn, g + 1)
                    src = bank[2][:, :]
                s.link(dve.tensor_tensor(per_tile(hn[:, :]), per_tile(src), spread(dinv, P), ALU.mult))
                s.link(dve.tensor_copy(s_hi[:, g * W:(g + 1) * W], hn[:, :]))
                s.link(dve.tensor_tensor(s_lo[:, g * W:(g + 1) * W], hn[:, :],
                                        s_hi[:, g * W:(g + 1) * W].bitcast(F32), ALU.subtract))
                s.done()

            def bn_norm(g):
                if g:
                    dve.wait_ge(s_bnturn, g)
                dve.tensor_scalar(outT[:, :], reg3[:, g * W:(g + 1) * W], bnmv[:, 0:1], bnmv[:, 5:6],
                                  ALU.subtract, ALU.mult).then_inc(s_bnnorm, 1)

            def take_sum(p, c, first, m=P):
                if p == "gat":
                    dve.wait_ge(s_gmm, c * T)
                else:
                    dve.wait_ge(s_mm[p], c * G)
                dve.wait_ge(s_half[p], c)
                if first:
                    if p == "agg1":
                        dve.wait_ge(s_bnturn, C)
                else:
                    dve.wait_ge(s_turn[p], c - 1)
                dve.tensor_tensor(outT[0:m, :], bank[1][0:m, :], half[0:m, :], ALU.add).then_inc(s_sum[p], 1)

            def agg_nodes_in(p, c, s):
                dinv = dinv0 if p == "agg0" else dinv1
                dve.wait_ge(s_turn[p], c)
                dve.wait_ge(s_hturn[p], c - 1)
                s.link(dve.tensor_tensor(hn[:, :], bank[2][:, :], s_hi[:, at(c, W, -W, W)].bitcast(F32), ALU.add))
                s.link(dve.tensor_tensor(hn[:, :], hn[:, :], s_lo[:, at(c, W, -W, W)].bitcast(F32), ALU.add))
                for q in range(Q):
                    xq = x[:, at(c, W, q * P - W, P)]
                    last = dve.scalar_tensor_tensor(xq, hn[:, q * P:(q + 1) * P], dinv[:, at(c, Q, q - Q, 1)],
                                                    xq, ALU.mult, ALU.add)
                s.link(last)
                norm_in(s, c - 1)

            def agg_project(p, c):
                if p == "agg0":
                    dve.wait_ge(s_pkeep[p], c)
                    dve.bn_stats(bnst[:, at(c, 6, -6, 6)], reg3[:, at(c, W, -W, W)]).then_inc(s_bnstat, 1)
                else:
                    dve.wait_ge(s_proj[p], c)
                    dve.tensor_copy(elr[:, at(c, 2 * Q, -2 * Q, 2 * Q)], bank[6][:, 0:2 * Q]).then_inc(s_pkeep[p], 1)

            for p in ("agg0", "agg1"):
                if p == "agg1":
                    s = Steps(dve, s_bn, 4, 0)
                    dve.wait_ge(s_bnstat, C)
                    s.link(dve.bn_aggr(bnmv[:, 0:2], bnst[:, :]))
                    s.inc(dve.tensor_scalar(bnmv[:, 2:3], bnmv[:, 1:2], float(N) / (N - 1), None, ALU.mult))
                    dve.wait_ge(s_bnroot, 1)
                    s.link(dve.tensor_scalar(bnmv[:, 4:5], bnmv[:, 3:4], 1.0e-6, None, ALU.add))
                    s.link(dve.reciprocal(bnmv[:, 5:6], bnmv[:, 4:5]))
                    s.done()
                    bn_norm(0)

                def agg_body(c, first, p=p):
                    if not first:
                        take_sum(p, c, isinstance(c, int) and c == 1)
                        s = Steps(dve, s_ln[p], LN_STEPS[p], c - 1)
                    for g in range(G):
                        if first:
                            if p == "agg1" and g + 1 < G:
                                bn_norm(g + 1)
                            scale(p, g)
                        dve.wait_ge(s_ahi[p], c * G + (g + 1))
                        dve.tensor_tensor(a_lo[:, ring_at(p, g)], ring[:, ring_at(p, g)],
                                          a_hi[:, (g % 4) * UNIT:(g % 4 + 1) * UNIT].bitcast(F32),
                                          ALU.subtract).then_inc(s_alo[p], 1)
                        if not first and g == 1:
                            agg_nodes_in(p, c, s)
                        if not first and g == 2:
                            s.inc(norm_out(s, p, c - 1, c))
                            s.done()
                        if not first and g == 6:
                            agg_project(p, c)
                over_chunks(dve, agg_body)
                take_sum(p, C, False)
                s = Steps(dve, s_ln[p], LN_STEPS[p], C - 1)
                agg_nodes_in(p, C, s)
                s.inc(norm_out(s, p, C - 1, C))
                s.done()
                agg_project(p, C)

            dve.wait_ge(s_e02, 2)
            dve.wait_ge(s_mm["agg1"], G * C)
            spv, smv = (a.rearrange("p (t e) -> p t e", e=ECOLS) for a in (sp_all, sm_all))
            dve.memset(spv[:, :, ECOLS - 1:ECOLS], 0.0)
            dve.memset(smv[:, :, ECOLS - 1:ECOLS], 1.0)

            def gat_nodes_in(c, s):
                e = el02[:, at(c, Q, -Q, Q)]
                dve.wait_ge(s_gden, c)
                dve.wait_ge(s_turn["gat"], c)
                s.link(dve.tensor_tensor(den[:, 0:Q], bank[7][:, 0:Q], e, ALU.mult))
                s.link(dve.tensor_scalar(den[:, Q:2 * Q], den[:, 0:Q], 1.0e-12, None, ALU.max))
                s.link(dve.reciprocal(den[:, 2 * Q:3 * Q], den[:, Q:2 * Q]))
                s.link(dve.tensor_tensor(den[:, 3 * Q:4 * Q], den[:, 2 * Q:3 * Q], e, ALU.mult))
                for q in range(Q):
                    xq = x[:, at(c, W, q * P - W, P)]
                    last = dve.scalar_tensor_tensor(xq, bank[2][:, q * P:(q + 1) * P],
                                                    den[:, 3 * Q + q:3 * Q + q + 1], xq, ALU.mult, ALU.add)
                s.link(last)
                xc = per_tile(x[:, at(c, W, -W, W)])
                s.link(dve.tensor_tensor(xc, xc, spread(b2all[:, :], Q, 1), ALU.add))
                norm_in(s, c - 1)

            def gat_nodes_out(c, s):
                dve.wait_ge(s_hturn["gat"], c - 1)
                s.link(norm_out(s, "gat", c - 1, c))
                s.link(dve.tensor_scalar(hn[:, :], hn[:, :], 0.0, None, ALU.max))
                s.inc(dve.tensor_copy(reg1[:, at(c, W, -W, W)], hn[:, :]))
                s.done()

            def gat_project(c):
                s = Steps(dve, s_pkeep["gat"], U_STEPS, c - 1)
                HS = Q * SCORES
                u, r = ucut[:, 0:HS], ucut[:, HS:2 * HS]
                uv, rv = (a.rearrange("p (t e) -> p t e", e=SCORES) for a in (u, r))
                spc, smc = (a[:, at(c, Q * ECOLS, -Q * ECOLS, Q * ECOLS)].rearrange("p (t e) -> p t e", e=ECOLS)
                            for a in (sp_all, sm_all))
                dve.wait_ge(s_proj["gat"], c)
                s.link(dve.tensor_copy(u, bank[4][:, 0:HS]))
                s.link(dve.tensor_copy(spc[:, :, 0:SCORES], uv))
                s.link(dve.tensor_tensor(rv, uv, spc[:, :, 0:SCORES], ALU.subtract))
                s.link(dve.tensor_copy(spc[:, :, SCORES:2 * SCORES], rv))
                s.link(dve.tensor_tensor(uv, rv, spc[:, :, SCORES:2 * SCORES], ALU.subtract))
                s.link(dve.tensor_copy(spc[:, :, 2 * SCORES:3 * SCORES], uv))
                for part in range(3):
                    a = part * SCORES
                    dve.tensor_copy(smc[:, :, a:a + HEADS], spc[:, :, a + HEADS:a + SCORES])
                    last = dve.tensor_copy(smc[:, :, a + HEADS:a + SCORES], spc[:, :, a:a + HEADS])
                s.inc(last)
                s.done()

            def gat_body(c, first):
                if not first:
                    take_sum("gat", c, False)
                    s = Steps(dve, s_ln["gat"], LN_STEPS["gat"], c - 1)
                for g in range(G):
                    dve.wait_ge(*loaded("gat", c, g))
                    mask = gmask[:, (g % 2) * UNIT:(g % 2 + 1) * UNIT]
                    dve.tensor_scalar(mask, ring[:, ring_at("gat", g)], 0.0, None,
                                      ALU.not_equal).then_inc(s_mask["gat"], 1)
                    dve.wait_ge(s_mask["gat"], c * G + (g + 1))
                    for q in range(Q):
                        m = g * Q + q
                        y = gtile[:, (m % GBUFS) * W:(m % GBUFS + 1) * W]
                        dve.wait_ge(s_gexp, c * T + (m + 1))
                        dve.scalar_tensor_tensor(y, y, er02[:, m:m + 1], mask[:, q * W:(q + 1) * W],
                                                 ALU.max, ALU.mult).then_inc(s_gy, 1)
                    if not first and g == 0:
                        dve.wait_ge(s_gden, c)
                    dve.wait_ge(s_gy, c * T + (g * Q + 1))
                    y = gtile[:, (g * Q % GBUFS) * W:(g * Q % GBUFS + 1) * W]
                    if g == 0:
                        dve.tensor_copy(den_v, y).then_inc(s_gdd, 1)
                    else:
                        dve.wait_ge(s_gdd, c * G + g)
                        dve.tensor_tensor(den_v, den_v, y, ALU.add).then_inc(s_gdd, 1)
                    if not first and g == 1:
                        gat_nodes_in(c, s)
                    if not first and g == 2:
                        gat_nodes_out(c, s)
                    if not first and g == 6:
                        gat_project(c)
            over_chunks(dve, gat_body)
            take_sum("gat", C, False)
            s = Steps(dve, s_ln["gat"], LN_STEPS["gat"], C - 1)
            gat_nodes_in(C, s)
            gat_nodes_out(C, s)
            gat_project(C)

            def clear_diagonal(p, c, g):
                def clear():
                    for q in range(Q):
                        z = ring[:, ring_at(p, g, q * W + q * P, P)]
                        last = dve.tensor_tensor(z, z, offdiag[:, :], ALU.mult)
                    last.then_inc(s_fix[p], 1)
                    dve.wait_ge(s_fix[p], g + 1)
                if isinstance(c, int):
                    if c == g:
                        clear()
                else:
                    hold(dve)
                    with dve.If(c == g):
                        clear()

            def masks(p, c, g, first):
                dve.wait_ge(*loaded(p, c, g))
                clear_diagonal(p, c, g)
                if g >= 2 or not first:
                    dve.wait_ge(s_mm[p], c * G + (g - 1))
                elif p == "edge":
                    dve.wait_ge(s_gdp, (T - G) * C)
                    dve.wait_ge(s_gmm, T * C)
                    dve.wait_ge(s_gden, C)
                src, dst = ring[:, ring_at(p, g)], slice((g % 2) * UNIT, (g % 2 + 1) * UNIT)
                dve.tensor_scalar(pmask[:, dst], src, 0.0, None, ALU.is_gt)
                dve.tensor_scalar(mmask[:, dst], src, 0.0, None, ALU.is_lt).then_inc(s_mask[p], 1)

            def edge_nodes(c):
                s = Steps(dve, s_ee, EDGE_STEPS, c - 1)
                dve.wait_ge(s_cut["edge"], c)
                ev = eraw[:, :].rearrange("p (t e) -> p t e", e=ECOLS)
                es = esum[:, :].rearrange("p (t e) -> p t e", e=SCORES)
                s.link(dve.tensor_tensor(es, ev[:, :, 2 * SCORES:3 * SCORES], ev[:, :, SCORES:2 * SCORES], ALU.add))
                s.link(dve.tensor_tensor(es, es, ev[:, :, 0:SCORES], ALU.add))
                ec = e6[:, at(c, Q * SCORES, -Q * SCORES, Q * SCORES)]
                s.link(dve.scalar_tensor_tensor(ec, esum[:, :], SLOPE, esum[:, :], ALU.mult, ALU.max))
                ec = ec.rearrange("p (t e) -> p t e", e=SCORES)
                nec, dec = (a[:, at(c, Q * HEADS, -Q * HEADS, Q * HEADS)].rearrange("p (t e) -> p t e", e=HEADS)
                            for a in (neg_e, d_e))
                dve.tensor_scalar(nec, ec[:, :, 0:HEADS], -1.0, None, ALU.mult)
                dve.tensor_tensor(dec, ec[:, :, HEADS:SCORES], ec[:, :, 0:HEADS], ALU.subtract)
                s.inc(dve.tensor_copy(cnt[:, at(c, Q, -Q, Q)].unsqueeze(2), ev[:, :, ECOLS - 1:ECOLS]))
                s.done()

            def edge_body(c, first):
                if not first:
                    take_sum("edge", c, False, ECOLS)
                for g in range(G):
                    masks("edge", c, g, first)
                    if not first and g == 3:
                        edge_nodes(c)
            over_chunks(dve, edge_body)
            take_sum("edge", C, False, ECOLS)
            edge_nodes(C)

            s = Steps(dve, s_prep, PREP_HEAD + 2 * PREP_SIGN, 0)
            dve.wait_ge(s_ee, C * EDGE_STEPS)
            dve.tensor_reduce(top[:, 0:HEADS], e6[:, :].rearrange("p (t h k) -> p k t h", h=2, k=HEADS),
                              AX.XY, ALU.max)
            s.inc(dve.tensor_reduce(top[:, HEADS:HEADS + 1], cnt[:, :], AX.X, ALU.max))
            dve.wait_ge(s_ptop, 1)
            H4 = HEADS + 1
            s.link(dve.tensor_reduce(top[0:H4, 4:5], bank[2][0:H4, 0:P], AX.X, ALU.max))
            s.inc(dve.tensor_scalar(top[0:H4, 8:8 + H4], ident[0:H4, 0:H4], top[0:H4, 4:5], None, ALU.mult))
            dve.wait_ge(s_ptop, 2)
            dve.tensor_scalar(flag[0:1, 0:1], bank[3][0:1, HEADS:H4], 0.0, None, ALU.is_gt).then_inc(s_flag, 1)
            s.link(dve.tensor_scalar(top[:, 12:12 + HEADS], bank[3][:, 0:HEADS], ROUND, None, ALU.add))
            s.link(dve.tensor_scalar(c0[:, 0:HEADS], top[:, 12:12 + HEADS], ROUND, 1.0, ALU.subtract, ALU.add))
            s.link(dve.tensor_scalar(c0[:, HEADS:2 * HEADS], c0[:, 0:HEADS], -1.0, None, ALU.mult))
            s.link(dve.tensor_scalar(c0[:, 2 * HEADS:3 * HEADS], c0[:, 0:HEADS], -(STEP * WINDOWS + LIFT), None, ALU.add))
            for k in range(HEADS):
                last = dve.tensor_scalar(shift[:, k * WINDOWS:(k + 1) * WINDOWS], wconst[:, 0:WINDOWS],
                                         c0[:, HEADS + k:HEADS + k + 1], None, ALU.add)
            s.link(last)
            dve.wait_ge(s_mm["edge"], G * C)
            dve.wait_ge(s_gmm, T * C)
            KW = HEADS * WINDOWS
            s.link(dve.memset(top[:, 16:17], 0.0))
            for sign, v in ((0, vp), (1, vm)):
                e_v = e6[:, :].rearrange("p (t h k) -> p t h k", h=2, k=HEADS)
                arg, capped, rest = (a.rearrange("p (t v) -> p t v", v=KW) for a in vtmp)
                parts = [v.rearrange("p (t v) -> p t v", v=VCOLS)[:, :, i * KW:(i + 1) * KW] for i in range(3)]
                for k in range(HEADS):
                    last = dve.tensor_tensor(arg[:, :, k * WINDOWS:(k + 1) * WINDOWS],
                                             e_v[:, :, sign, k:k + 1].to_broadcast([P, T, WINDOWS]),
                                             shift[:, k * WINDOWS:(k + 1) * WINDOWS].unsqueeze(1)
                                             .to_broadcast([P, T, WINDOWS]), ALU.add)
                s.link(last)
                s.inc(dve.tensor_scalar(vtmp[1], vtmp[0], LIFT, None, ALU.min))
                dve.wait_ge(s_vexp, sign + 1)
                s.link(dve.scalar_tensor_tensor(vtmp[2], vtmp[0], LIFT, vtmp[1], ALU.is_le, ALU.mult))
                s.link(dve.tensor_copy(parts[0], rest))
                s.link(dve.tensor_tensor(rest, rest, parts[0], ALU.subtract))
                s.link(dve.tensor_copy(parts[1], rest))
                s.link(dve.tensor_tensor(rest, rest, parts[1], ALU.subtract))
                s.link(dve.tensor_copy(parts[2], rest))
            s.done()

            def norm_nodes_in(c, s):
                def g_at(i):
                    return gd[:, i * Q * HEADS:(i + 1) * Q * HEADS]

                def win(a):
                    return a.rearrange("p (n b) -> p n b", b=WINDOWS)
                dve.wait_ge(s_cut["norm"], c)
                vv = vcut.rearrange("p (t v) -> p t v", v=VCOLS)
                dv = dsum.rearrange("p (t v) -> p t v", v=KW)
                s.link(dve.tensor_tensor(dv, vv[:, :, 2 * KW:3 * KW], vv[:, :, KW:2 * KW], ALU.add))
                s.link(dve.tensor_tensor(dv, dv, vv[:, :, 0:KW], ALU.add))
                s.link(dve.tensor_scalar(dok, dsum, WINDOW_MIN, None, ALU.is_ge))
                s.link(dve.tensor_tensor(win(dwin), win(dok), spread(wconst[:, WINDOWS:2 * WINDOWS], Q * HEADS, 1), ALU.mult))
                s.link(dve.tensor_reduce(g_at(0), win(dwin), AX.X, ALU.max))
                s.link(dve.tensor_tensor(win(dsel), win(dwin), spread(g_at(0), WINDOWS), ALU.is_equal))
                s.link(dve.tensor_tensor(dsel, dsel, dok, ALU.mult))
                s.link(dve.tensor_tensor(dsel, dsel, dsum, ALU.mult))
                s.link(dve.tensor_reduce(g_at(1), win(dsel), AX.X, ALU.add))
                s.link(dve.tensor_scalar(g_at(2), g_at(0), STEP, None, ALU.mult))
                g2 = g_at(2).rearrange("p (t k) -> p t k", k=HEADS)
                s.link(dve.tensor_tensor(g2, g2, spread(c0[:, 2 * HEADS:3 * HEADS], Q, 1), ALU.add))
                s.link(dve.tensor_scalar(g_at(3), g_at(1).bitcast(I32), LN2 / 2 ** 23, 0.1 - 127 * LN2,
                                         ALU.mult, ALU.add))
                s.link(dve.tensor_tensor(g_at(6), g_at(2), g_at(3), ALU.add))
                s.inc(dve.tensor_tensor(g_at(4), g_at(2), g_at(6), ALU.subtract))

            def norm_nodes_out(c, s):
                def g_at(i):
                    return gd[:, i * Q * HEADS:(i + 1) * Q * HEADS]
                dve.wait_ge(s_nexp, c)
                s.link(dve.tensor_tensor(g_at(0), g_at(1), g_at(5), ALU.mult))
                s.link(dve.tensor_scalar(g_at(0), g_at(0), 1.0e-30, None, ALU.max))
                dve.wait_ge(s_nturn, c - 1)
                nv = nr[:, :].rearrange("p (t e) -> p t e", e=SCORES)
                dve.tensor_scalar(nv[:, :, 0:HEADS], g_at(6).rearrange("p (t k) -> p t k", k=HEADS),
                                  -1.0, None, ALU.mult)
                s.inc(dve.reciprocal(nv[:, :, HEADS:SCORES], g_at(0).rearrange("p (t k) -> p t k", k=HEADS)))
                s.done()

            def norm_body(c, first):
                if not first:
                    take_sum("norm", c, False, VCOLS)
                    s = Steps(dve, s_ne, NORM_STEPS, c - 1)
                for g in range(G):
                    masks("norm", c, g, first)
                    if not first and g == 2:
                        norm_nodes_in(c, s)
                    if not first and g == 3:
                        norm_nodes_out(c, s)
            over_chunks(dve, norm_body)
            take_sum("norm", C, False, VCOLS)
            s = Steps(dve, s_ne, NORM_STEPS, C - 1)
            norm_nodes_in(C, s)
            norm_nodes_out(C, s)

            negative = dve.value_load(flag[0:1, 0:1], min_val=0, max_val=1)

            def take_chunk(c):
                dve.wait_ge(s_mm["out"], c * G)
                dve.wait_ge(s_rrk, c)
                dve.wait_ge(s_es, c - 1)
                dve.wait_ge(s_gm, c * 2 - 2)
                dve.tensor_copy(nsT, bank[0][:, :])
                for k in range(HEADS):
                    last = dve.tensor_tensor(nk[:, k * W:(k + 1) * W], bank[1 + k][:, :],
                                             rden[:, k * W:(k + 1) * W], ALU.mult)
                last.then_inc(s_nk, 1)

            def cell_in(c, cell, s):
                dve.wait_ge(s_ga, c * 4 + (2 * cell - 3))
                s.link(dve.tensor_scalar(gr, gr, 0.5, 0.5, ALU.mult, ALU.add))
                s.link(dve.scalar_tensor_tensor(gt, bank[7][:, :], gb[:, 4 * cell + 3:4 * cell + 4], gr,
                                                ALU.add, ALU.mult))
                s.inc(dve.scalar_tensor_tensor(gt, bank[4][:, :], gb[:, 4 * cell + 2:4 * cell + 3], gt,
                                               ALU.add, ALU.add))

            def cell_out_steps(c, cell, s):
                dve.wait_ge(s_ga, c * 4 + (2 * cell - 2))
                s.link(dve.tensor_tensor(gr, reg2[:, at(c, W, -W, W)], gn, ALU.subtract))
                s.link(dve.scalar_tensor_tensor(gr, gz, 1.0, gr, ALU.add, ALU.mult))
                if cell == 0:
                    s.link(dve.scalar_tensor_tensor(cell_out, gr, 0.5, gn, ALU.mult, ALU.add))
                else:
                    dve.wait_ge(s_ot, c - 1)
                    s.link(dve.scalar_tensor_tensor(cells, gr, 0.5, gn, ALU.mult, ALU.add))
                    s.inc(dve.tensor_tensor(cells, cells, cell_out, ALU.add))
                    s.done()

            def result(c):
                dve.wait_ge(s_ot, c)
                dve.wait_ge(s_store, c * 16 - 16)
                for q in range(Q):
                    last = dve.scalar_tensor_tensor(res[:, q * P:(q + 1) * P], bank[5][:, q * P:(q + 1) * P],
                                                    diag[:, at(c, Q, q - Q, 1)], x[:, at(c, W, q * P - W, P)],
                                                    ALU.mult, ALU.add)
                last.then_inc(s_res, 1)

            def negative_exponents(c, g, first):
                if g == 0:
                    dve.wait_ge(s_ggk, c + 1)
                s = Steps(dve, s_slow, G * (1 + Q * HEADS), c)
                s.n = g * (1 + Q * HEADS)
                s.link(dve.tensor_scalar(nmask, ring[:, ring_at("out", g)], 0.0, None, ALU.is_lt))
                for m in range(g * Q * HEADS, (g + 1) * Q * HEADS):
                    t, k = m // HEADS, m % HEADS
                    s.link(dve.scalar_tensor_tensor(slow, nmask[:, (t % Q) * W:(t % Q + 1) * W],
                                                    d_e[:, t * HEADS + k:t * HEADS + k + 1],
                                                    negg[:, k * W:(k + 1) * W], ALU.mult, ALU.add))
                    if m >= BUFS or not first:
                        dve.wait_ge(s_used, c * (T * HEADS) + (m + 1 - BUFS))
                    dve.tensor_scalar(tile[:, (m % BUFS) * W:(m % BUFS + 1) * W], slow,
                                      neg_e[:, t * HEADS + k:t * HEADS + k + 1], None,
                                      ALU.min).then_inc(s_clamp, 1)

            def out_body(c, first, negatives):
                if not first:
                    s = Steps(dve, s_gv, CELL_STEPS, c - 1)
                for g in range(G):
                    dve.wait_ge(*loaded("out", c, g))
                    clear_diagonal("out", c, g)
                    if negatives:
                        if not first and g == 0:
                            take_chunk(c)
                        negative_exponents(c, g, first)
                    for q in range(Q):
                        for k in range(HEADS):
                            m = (g * Q + q) * HEADS + k
                            y = tile[:, (m % BUFS) * W:(m % BUFS + 1) * W]
                            dve.wait_ge(s_exp, c * (T * HEADS) + (m + 1))
                            dve.tensor_tensor(y, y, ring[:, ring_at("out", g, q * W, W)], ALU.mult).then_inc(s_y, 1)
                        if not first and not negatives and g == 0 and q == 0:
                            take_chunk(c)
                    if not first:
                        if g == 1:
                            cell_in(c, 0, s)
                        if g == 2:
                            cell_out_steps(c, 0, s)
                        if g == 4:
                            cell_in(c, 1, s)
                        if g == 5:
                            cell_out_steps(c, 1, s)
                        if g == 6:
                            result(c)

            with dve.If(negative == 0):
                over_chunks(dve, lambda c, first: out_body(c, first, False))
            with dve.Else():
                over_chunks(dve, lambda c, first: out_body(c, first, True))
            take_chunk(C)
            s = Steps(dve, s_gv, CELL_STEPS, C - 1)
            for cell in range(2):
                cell_in(C, cell, s)
                cell_out_steps(C, cell, s)
            result(C)

        @block.tensor
        def _(pe):
            def turn(dst, src, m=P):
                for q in range(Q):
                    last = pe.transpose(dst[:, q * m:(q + 1) * m], src[0:m, q * P:(q + 1) * P], ident[0:m, 0:m])
                return last

            pe.wait_ge(s_const, 16 * 5)
            pe.wait_ge(s_pc, 4)
            pe.matmul(bank[6][:, 0:P], ones[0:1, :], rows[0:1, P:2 * P], start=True, stop=True)
            pe.matmul(bank[7][:, 0:2], w2t, cols[:, 1:3], start=True, stop=True)
            for k in range(HEADS):
                last = pe.matmul(bank[7][:, 2 + 2 * k:4 + 2 * k], gat_wt[k], cols[:, 3 + 2 * k:5 + 2 * k],
                                 start=True, stop=True)
            last.then_inc(s_pw, 1)

            def turn_h(p, c):
                pe.wait_ge(s_ln[p], c * LN_STEPS[p])
                if not (isinstance(c, int) and c == 1):
                    pe.wait_ge(s_hT[p], c - 1)
                elif p != "deg":
                    pe.wait_ge(s_hT[NODE[NODE.index(p) - 1]], C)
                if p == "gat":
                    pe.wait_ge(s_hall, c - 1) if not (isinstance(c, int) and c == 1) else None
                turn(bank[3], hn).then_inc(s_hturn[p], 1)

            def project(p, c):
                pe.wait_ge(s_hT[p], c)
                if p == "deg":
                    if not (isinstance(c, int) and c == 1):
                        pe.wait_ge(s_pkeep[p], c - 1)
                    for q in range(Q):
                        o = bank[4][:, q * P:(q + 1) * P]
                        pe.matmul(o, ones[0:1, :], rows[0:1, 0:P], start=True, stop=False)
                        last = pe.matmul(o, hT[:, q * P:(q + 1) * P], w0t, start=False, stop=True)
                elif p == "agg0":
                    pe.wait_ge(s_pkeep["deg"], C)
                    pe.wait_ge(s_pkeep[p], c - 1)
                    last = pe.matmul(bank[4][:, :], w1t, hT[:, :], start=True, stop=True)
                elif p == "agg1":
                    pe.wait_ge(s_pkeep["agg0"], C)
                    pe.wait_ge(s_dw, 2)
                    pe.wait_ge(s_pkeep[p], c - 1)
                    pe.wait_ge(s_pkeep_act, c - 1)
                    pe.matmul(bank[5][:, :], wel[:, :], hT[:, :], start=True, stop=True)
                    for q in range(Q):
                        pe.matmul(bank[6][:, 2 * q:2 * q + 2], hT[:, q * P:(q + 1) * P], wlr[:, :],
                                  start=True, stop=True)
                    for q in range(Q):
                        last = pe.matmul(bank[4][:, q * P:(q + 1) * P], hT[:, q * P:(q + 1) * P], w2,
                                         start=True, stop=True)
                else:
                    pe.wait_ge(s_pkeep_act, C)
                    pe.wait_ge(s_pkeep[p], (c - 1) * U_STEPS)
                    for q in range(Q):
                        last = pe.matmul(bank[4][:, q * SCORES:(q + 1) * SCORES], hT[:, q * P:(q + 1) * P],
                                         wa[:, :], start=True, stop=True)
                last.then_inc(s_proj[p], 1)

            def deg_body(c, first):
                turn_h("deg", c + 1)
                project("deg", c + 1)
            pe.wait_ge(s_ln["deg"], LN_STEPS["deg"])
            turn(bank[3], hn).then_inc(s_hturn["deg"], 1)
            project("deg", 1)
            with pe.Fori(2, C + 1) as c:
                turn_h("deg", c)
                project("deg", c)

            def turn_sum(p, c, m=P):
                pe.wait_ge(s_sum[p], c)
                if p in ("edge", "norm"):
                    if not (isinstance(c, int) and c == 1):
                        pe.wait_ge(s_cut[p], c - 1)
                    else:
                        pe.wait_ge(s_ln["gat"], C * LN_STEPS["gat"])
                else:
                    pe.wait_ge(s_ln[p], (c - 1) * LN_STEPS[p])
                hold(pe)
                turn(bank[2], outT, m).then_inc(s_turn[p], 1)

            def accumulator(p, c, first, g):
                if g == 0:
                    if not first:
                        pe.wait_ge(s_half[p], c)
                    elif p != "agg0":
                        pe.wait_ge(s_half[PASSES[PASSES.index(p) - 1]], C)
                if g == G // 2:
                    if not first:
                        pe.wait_ge(s_sum[p], c)
                    elif p != "agg0":
                        pe.wait_ge(s_sum[PASSES[PASSES.index(p) - 1]], C)
                return bank[g // (G // 2)]

            def limits(g, q):
                return (g % (G // 2) == 0 and q == 0), (g % (G // 2) == G // 2 - 1 and q == Q - 1)

            for p in ("agg0", "agg1"):
                def turn_bn(g):
                    pe.wait_ge(s_bnnorm, g + 1)
                    if g:
                        pe.wait_ge(s_scale["agg1"], 3 * (g - 1) + 1)
                    else:
                        pe.wait_ge(s_ln["agg0"], C * LN_STEPS["agg0"])
                    turn(bank[2], outT).then_inc(s_bnturn, 1)

                def agg_body(c, first, p=p):
                    for g in range(G):
                        acc = accumulator(p, c, first, g)
                        if first:
                            if p == "agg1" and g == 0:
                                turn_bn(0)
                            if p == "agg1" and g + 1 < G:
                                turn_bn(g + 1)
                            pe.wait_ge(s_scale[p], 3 * (g + 1))
                        pe.wait_ge(s_alo[p], c * G + (g + 1))
                        for q in range(Q):
                            t = g * Q + q
                            begin, end = limits(g, q)
                            hi = a_hi[:, (g % 4) * UNIT + q * W:(g % 4) * UNIT + (q + 1) * W]
                            lo = a_lo[:, ring_at(p, g, q * W, W)]
                            sh, sl = s_hi[:, t * P:(t + 1) * P], s_lo[:, t * P:(t + 1) * P]
                            pe.matmul(acc[:, :], sh, hi, start=begin, stop=False)
                            pe.matmul(acc[:, :], sh, lo, start=False, stop=False)
                            last = pe.matmul(acc[:, :], sl, hi, start=False, stop=end)
                        last.then_inc(s_mm[p], 1)
                        if not first:
                            if g == 0:
                                turn_sum(p, c)
                            if g == 3:
                                turn_h(p, c)
                            if g == 5:
                                project(p, c)
                over_chunks(pe, agg_body)
                turn_sum(p, C)
                turn_h(p, C)
                project(p, C)

            pe.wait_ge(s_pkeep_act, C)

            def gat_body(c, first):
                for g in range(G):
                    acc = accumulator("gat", c, first, g)
                    for q in range(Q):
                        m = g * Q + q
                        begin, end = limits(g, q)
                        pe.wait_ge(s_gy, c * T + (m + 1))
                        last = pe.matmul(acc[:, :], reg3[:, m * P:(m + 1) * P],
                                         gtile[:, (m % GBUFS) * W:(m % GBUFS + 1) * W], start=begin, stop=end)
                        last.then_inc(s_gmm, 1)
                    if not first:
                        if g == 0:
                            turn_sum("gat", c)
                        if g == 3:
                            turn_h("gat", c)
                        if g == 5:
                            project("gat", c)
                pe.wait_ge(s_gdd, c * G + G)
                pe.wait_ge(s_gdp, c * (T - G) + (T - G))
                if not first:
                    pe.wait_ge(s_ln["gat"], c * LN_STEPS["gat"])
                for q in range(Q):
                    o = bank[7][:, q:q + 1]
                    pe.matmul(o, den_v[:, q * P:(q + 1) * P], ones[:, 0:1], start=True, stop=False)
                    last = pe.matmul(o, den_p[:, q * P:(q + 1) * P], ones[:, 0:1], start=False, stop=True)
                last.then_inc(s_gden, 1)
            over_chunks(pe, gat_body)
            turn_sum("gat", C)
            turn_h("gat", C)
            project("gat", C)

            def masked(p, m, plus, minus, extra):
                def body(c, first):
                    for g in range(G):
                        acc = accumulator(p, c, first, g)
                        pe.wait_ge(s_mask[p], c * G + (g + 1))
                        for q in range(Q):
                            t = g * Q + q
                            begin, end = limits(g, q)
                            o = (g % 2) * UNIT + q * W
                            pe.matmul(acc[0:m, :], plus[:, t * m:(t + 1) * m], pmask[:, o:o + W],
                                      start=begin, stop=False)
                            last = pe.matmul(acc[0:m, :], minus[:, t * m:(t + 1) * m], mmask[:, o:o + W],
                                             start=False, stop=end)
                        last.then_inc(s_mm[p], 1)
                        if not first:
                            if g == 0:
                                turn_sum(p, c, m)
                            extra(c, g)
                return body

            pe.wait_ge(s_pkeep["gat"], C * U_STEPS)
            over_chunks(pe, masked("edge", ECOLS, sp_all, sm_all, lambda c, g: None))
            turn_sum("edge", C, ECOLS)

            pe.wait_ge(s_prep, 1)
            pe.wait_ge(s_cut["edge"], C)
            pe.transpose(bank[2][0:HEADS + 1, 0:P], top[:, 0:HEADS + 1], ident[:, :]).then_inc(s_ptop, 1)
            pe.wait_ge(s_prep, 3)
            pe.matmul(bank[3][:, 0:HEADS + 1], ones[0:HEADS + 1, :], top[0:HEADS + 1, 8:9 + HEADS],
                      start=True, stop=True).then_inc(s_ptop, 1)
            pe.wait_ge(s_prep, PREP_HEAD + 2 * PREP_SIGN)

            def turn_rows(c):
                pe.wait_ge(s_ne, c * NORM_STEPS)
                if not (isinstance(c, int) and c == 1):
                    pe.wait_ge(s_nrow, c - 1)
                for q in range(Q):
                    last = pe.transpose(bank[3][0:SCORES, q * P:(q + 1) * P],
                                        nr[:, q * SCORES:(q + 1) * SCORES], ident[:, :])
                last.then_inc(s_nturn, 1)

            over_chunks(pe, masked("norm", VCOLS, vp, vm, lambda c, g: turn_rows(c) if g == 5 else None))
            turn_sum("norm", C, VCOLS)
            turn_rows(C)

            def spread_rows(c, first_row, banks):
                for k in range(HEADS):
                    r = first_row + k
                    last = pe.matmul(bank[banks[k]][:, :], pick[:, r * P:(r + 1) * P], grows[:, at(c, W, 0, W)],
                                     start=True, stop=True)
                return last

            def gates(c, cell, src):
                h = reg2[:, at(c, W, -W, W)]
                for gate, b in ((0, 5), (1, 6)):
                    pe.matmul(bank[b][:, :], gate_w(cell, 0, gate), src, start=True, stop=False)
                    pe.matmul(bank[b][:, :], gate_w(cell, 1, gate), h, start=False, stop=True)
                pe.matmul(bank[7][:, :], gate_w(cell, 1, 2), h, start=True, stop=True)
                pe.matmul(bank[4][:, :], gate_w(cell, 0, 2), src, start=True, stop=True).then_inc(s_gm, 1)

            def edge_gates(c):
                pe.wait_ge(s_nk, c)
                pe.wait_ge(s_ggk, c + 1)
                pe.wait_ge(s_res, c - 1)
                gates(c, 0, nsT)

            def heads(c):
                pe.wait_ge(s_gv, c * CELL_STEPS + (CELL_A - CELL_STEPS))
                for k in range(HEADS):
                    last = pe.matmul(bank[4][:, :], gat_w[k], nk[:, k * W:(k + 1) * W],
                                     start=(k == 0), stop=(k == HEADS - 1))
                last.then_inc(s_es, 1)

            def spread_dens(c, first):
                if not first:
                    pe.wait_ge(s_gv, c * CELL_STEPS + (CELL_A - CELL_STEPS))
                    pe.wait_ge(s_ga, c * 4 - 3)
                else:
                    pe.wait_ge(s_ggk, 1)
                spread_rows(c, HEADS, (5, 6, 7)).then_inc(s_rr, 1)

            def node_gates(c, last_chunk):
                pe.wait_ge(s_esk, c)
                if not last_chunk:
                    pe.wait_ge(s_rrk, c + 1)
                gates(c, 1, esT)

            def turn_cells(c):
                pe.wait_ge(s_gv, c * CELL_STEPS)
                turn(bank[5], cells).then_inc(s_ot, 1)

            def spread_guards(c, first):
                if not first:
                    pe.wait_ge(s_gv, c * CELL_STEPS + (CELL_B + CELL_A - CELL_STEPS))
                else:
                    pe.wait_ge(s_rrk, 1)
                spread_rows(c + 1, 0, (4, 6, 7)).then_inc(s_gg, 1)

            pe.wait_ge(s_nrow, C)
            spread_rows(0, 0, (4, 6, 7)).then_inc(s_gg, 1)

            def out_body(c, first):
                for g in range(G):
                    for q in range(Q):
                        t = g * Q + q
                        begin, end = t == 0, t == T - 1
                        h = reg1[:, t * P:(t + 1) * P]
                        if begin and not first:
                            pe.wait_ge(s_nk, c)
                        for k in range(HEADS):
                            m = t * HEADS + k
                            pe.wait_ge(s_y, c * (T * HEADS) + (m + 1))
                            pe.matmul(bank[1 + k][:, :], h, tile[:, (m % BUFS) * W:(m % BUFS + 1) * W],
                                      start=begin, stop=end).then_inc(s_used, 1)
                        last = pe.matmul(bank[0][:, :], h, ring[:, ring_at("out", g, q * W, W)],
                                         start=begin, stop=end)
                    last.then_inc(s_mm["out"], 1)
                    if not first:
                        if g == 0:
                            edge_gates(c)
                        if g == 1:
                            heads(c)
                        if g == 3:
                            node_gates(c, False)
                        if g == 5:
                            turn_cells(c)
                    if g == 1:
                        spread_dens(c, first)
                    if g == 6:
                        spread_guards(c, first)
            over_chunks(pe, out_body)
            edge_gates(C)
            heads(C)
            node_gates(C, True)
            turn_cells(C)


def kernel(x, adj, L0_gnn_W, L0_gnn_b, L1_gnn_W, L1_gnn_b, L2_gnn_weight, L2_gnn_a_l, L2_gnn_a_r, L2_gnn_b,
           L3_gnn_gat_W, L3_gnn_gat_a, L3_gnn_edge_Wih, L3_gnn_edge_Whh, L3_gnn_edge_bih, L3_gnn_edge_bhh,
           L3_gnn_node_Wih, L3_gnn_node_Whh, L3_gnn_node_bih, L3_gnn_node_bhh):
    import numpy as np
    import concourse.bacc as bacc
    from concourse.bass_utils import run_bass_kernel_spmd

    x, adj = np.asarray(x), np.asarray(adj)
    gat_w, gat_a = np.asarray(L3_gnn_gat_W), np.asarray(L3_gnn_gat_a)

    def turned(a):
        return np.asarray(a).T

    units = adj.T.reshape(G, Q, P, C, W).transpose(3, 0, 2, 1, 4).reshape(C * G * P, UNIT)
    weights = np.concatenate(
        [turned(L0_gnn_W), turned(L1_gnn_W), np.asarray(L2_gnn_weight), turned(L2_gnn_weight)]
        + [gat_w[k] for k in range(HEADS)] + [gat_w[k].T for k in range(HEADS)], axis=1)
    cells = np.concatenate([turned(w) for w in (L3_gnn_edge_Wih, L3_gnn_edge_Whh, L3_gnn_node_Wih,
                                                L3_gnn_node_Whh)], axis=1)
    columns = np.stack(
        [np.asarray(a) for a in (L1_gnn_b, L2_gnn_a_l, L2_gnn_a_r)]
        + [gat_a[k, h * P:(h + 1) * P, 0] for k in range(HEADS) for h in range(2)]
        + [np.asarray(b)[g * P:(g + 1) * P] for b in (L3_gnn_edge_bih, L3_gnn_edge_bhh, L3_gnn_node_bih,
                                                      L3_gnn_node_bhh) for g in range(3)], axis=1)
    row_pair = np.concatenate([np.asarray(L0_gnn_b), np.asarray(L2_gnn_b)])[None, :]
    arrays = {
        "in_x": x,
        "in_adj_rows": adj,
        "in_adj_units": units,
        "in_adj_diag": np.diagonal(adj).reshape(T, P).T,
        "in_weights": weights,
        "in_cells": cells,
        "in_columns": columns,
        "in_rows": row_pair,
    }
    arrays = {name: np.ascontiguousarray(a) for name, a in arrays.items()}
    nc = bacc.Bacc("TRN2", target_bir_lowering=False, num_devices=1)
    args = [nc.dram_tensor(name, a.shape, F32, kind="ExternalInput").ap() for name, a in arrays.items()]
    out = nc.dram_tensor("out", (N, P), F32, kind="ExternalOutput").ap()
    build(nc, *args, out)
    return run_bass_kernel_spmd(nc, [arrays], core_ids=[0]).results[0]["out"]
```

```python
from contextlib import ExitStack

import concourse.bass as bass
from concourse import mybir
from concourse.alu_op_type import AluOpType as ALU

ACT = mybir.ActivationFunctionType
AX = mybir.AxisListType
F32 = mybir.dt.float32
F32R = mybir.dt.float32r
BF16 = mybir.dt.bfloat16
I32 = mybir.dt.int32

P = 128
N = 4096
T = N // P
W = 512
C = N // W
Q = W // P
G = T // Q
POOL_UNITS = (1, 4, 6)
DVE_UNITS = tuple(g for g in range(G) if g not in POOL_UNITS)
UNIT = Q * W
HEADS = 3
EPS = 1e-5
SLOPE = 0.2
LN2 = 0.6931471805599453

WINDOWS = P // (3 * HEADS)
STEP = 120.0
LIFT = 78.0
VCOLS = 3 * HEADS * WINDOWS
ECOLS = 3 * 2 * HEADS + 1
SCORES = 2 * HEADS
RING_OUT = 4
GROUPS = 4
AHEAD = 2
GBUFS = 3
WINDOW_MIN = 2.3e-19
ROUND = 12582912.0

LN_STEPS = {"deg": 5, "agg0": 8, "agg1": 8, "gat": 13}
LN_ROOT = {"deg": 3, "agg0": 6, "agg1": 6, "gat": 9}
U_STEPS = 7
EDGE_STEPS = 4
NORM_STEPS, NORM_EXP = 17, 14
PREP_HEAD, PREP_SIGN = 9, 8
SLOW_STEPS = 2 * HEADS
CELL_A, CELL_B = 3, 6
CELL_STEPS = 2 * CELL_B + 1


def at(c, step, off, size):
    if isinstance(c, int):
        return slice(step * c + off, step * c + off + size)
    return bass.ds(c * step + off, size)


class Steps:

    def __init__(self, eng, sem, k, c):
        self.eng, self.sem, self.k, self.base, self.n = eng, sem, k, c * k, 0

    def inc(self, instruction):
        self.n += 1
        instruction.then_inc(self.sem, 1)

    def link(self, instruction):
        self.inc(instruction)
        self.eng.wait_ge(self.sem, self.base + self.n)

    def done(self):
        assert self.n == self.k, (self.sem, self.n)


def over_chunks(eng, body):
    body(0, True)
    with eng.Fori(1, C) as c:
        body(c, False)


def over_chunks_deep(eng, body):
    body(0, False, False)
    body(1, True, False)
    with eng.Fori(2, C) as c:
        body(c, True, True)


def build(nc, x_d, rows_d, cols_d, diag_d, w_d, gru_d, col_d, row_d, out_d):
    with ExitStack() as ctx:
        def sb(name, shape, dt=F32):
            return ctx.enter_context(nc.sbuf_tensor(name, shape, dt))

        def sem(name):
            return ctx.enter_context(nc.semaphore(name))

        def shared(name, shape, dt):
            with nc.sbuf_tensor(name, shape, dt) as view:
                return view

        bank = [ctx.enter_context(nc.psum_tensor(f"bank{i}", [P, W], F32)) for i in range(8)]

        a_lo = shared("a_lo", [P, G * UNIT], F32R)
        ring = sb("ring", [P, G * UNIT])
        x = sb("x", [P, N])
        s_hi = shared("s_hi", [P, N], F32R)
        reg1 = sb("reg1", [P, N])
        s_lo = shared("s_lo", [P, N], F32R)
        reg2 = sb("reg2", [P, N])
        reg3 = sb("reg3", [P, N])
        reg4 = sb("reg4", [P, N + W])
        a_hi = shared("a_hi", [P, 8192], F32R)
        work = sb("work", [P, 8192])
        half = sb("half", [P, W])
        outT = sb("outT", [P, W])
        hn = sb("hn", [P, W])
        hT = sb("hT", [P, W])
        wts = sb("wts", [P, 10 * P])
        gru = sb("gru", [P, 4 * 3 * P])
        cols = sb("cols", [P, 21])
        diag = sb("diag", [P, T])
        ident = sb("ident", [P, P])
        ones = sb("ones", [P, P])
        offdiag = sb("offdiag", [P, P])
        pick = sb("pick", [SCORES, SCORES * P])
        b2all = sb("b2all", [P, P])
        wel = sb("wel", [P, P])
        wlr = sb("wlr", [P, 2])
        wa = sb("wa", [P, SCORES])
        gb = sb("gb", [P, 8])
        dinv0 = sb("dinv0", [P, T])
        dinv1 = sb("dinv1", [P, T])
        stats = sb("stats", [P, Q * 6])
        mv = sb("mv", [P, Q * 2])
        rstd = sb("rstd", [P, 3 * Q])
        bnst = sb("bnst", [P, C * 6])
        bnmv = sb("bnmv", [P, 6])
        elr = sb("elr", [P, 2 * T])
        el02 = sb("el02", [P, T])
        er02 = sb("er02", [P, T])
        er08 = sb("er08", [P, T])
        den = sb("den", [P, 4 * Q])
        esum = sb("esum", [P, Q * SCORES])
        e6 = sb("e6", [P, T * SCORES])
        d_e = sb("d_e", [P, T * HEADS])
        cnt = sb("cnt", [P, T])
        top = sb("top", [P, 20])
        flag = sb("flag", [1, 1], I32)
        c0 = sb("c0", [P, 3 * HEADS])
        wconst = sb("wconst", [P, 2 * WINDOWS])
        shift = sb("shift", [P, HEADS * WINDOWS])
        gd = sb("gd", [P, 7 * Q * HEADS])
        nr = sb("nr", [P, Q * SCORES])

        w0t, w1t, w2, w2t = (wts[:, i * P:(i + 1) * P] for i in range(4))
        gat_w = [wts[:, (4 + k) * P:(5 + k) * P] for k in range(HEADS)]
        gat_wt = [wts[:, (7 + k) * P:(8 + k) * P] for k in range(HEADS)]

        def gate_w(cell, hidden, gate):
            i = (2 * cell + hidden) * 3 + gate
            return gru[:, i * P:(i + 1) * P]

        rows = reg4[0:1, 0:2 * P]
        degp = reg4[:, 512:512 + 2 * T]
        deg = reg4[:, 1024:1024 + 7 * T]

        def gunit(g):
            b = g % GBUFS
            return work[:, b * UNIT:(b + 1) * UNIT]

        def gat_user(g):
            return g - GBUFS + 1 if g >= GBUFS else max(u for u in range(G) if u % GBUFS == g) + 1 - G

        den_v, den_p = work[:, 6144:6144 + W], work[:, 6656:6656 + W]
        SP, ER = 7168, 7168 + T * ECOLS
        sp_all = work[:, SP:SP + T * ECOLS // 2].bitcast(BF16)
        sm_all = work[:, SP + T * ECOLS // 2:ER].bitcast(BF16)
        eraw = work[:, ER:ER + Q * ECOLS]
        ucut = work[:, ER + Q * ECOLS:ER + Q * ECOLS + 2 * Q * SCORES]
        pmask = work[:, 0:UNIT].bitcast(BF16)
        mmask = work[:, UNIT:2 * UNIT].bitcast(BF16)
        vcut = work[:, 4096:4096 + Q * VCOLS]
        VB = Q * HEADS * WINDOWS
        dsum, dok, dwin, dsel = (work[:, 4608 + i * VB:4608 + (i + 1) * VB] for i in range(4))
        VT = T * HEADS * WINDOWS
        vtmp = [work[:, i * VT:(i + 1) * VT] for i in range(3)]
        negg = work[:, GROUPS * HEADS * W:(GROUPS + 1) * HEADS * W]

        def tiles(t):
            b = t % GROUPS
            return work[:, b * HEADS * W:(b + 1) * HEADS * W]

        vp = reg3[:, 0:T * VCOLS // 2].bitcast(BF16)
        vm = reg3[:, N // 2:N // 2 + T * VCOLS // 2].bitcast(BF16)
        grows = reg4[0:SCORES, :]
        spare = ring[:, RING_OUT * UNIT:G * UNIT]
        rden = spare[:, 0:HEADS * W]
        nk = spare[:, 3 * W:6 * W]
        nsT, esT = spare[:, 6 * W:7 * W], spare[:, 7 * W:8 * W]
        gr, gz, gn, gt = (spare[:, (8 + i) * W:(9 + i) * W] for i in range(4))
        cell_out = spare[:, 12 * W:13 * W]
        cells = spare[:, 13 * W:14 * W]
        res = spare[:, 14 * W:15 * W]
        slow = spare[:, 15 * W:16 * W]
        nmask = reg3[:, 0:W]

        s_passed = sem("waits_passed")
        s_const, s_xin = sem("constants_loaded"), sem("x_loaded")
        s_rows = [sem(f"row_tile_loaded{i}") for i in range(4)]
        s_unit = [sem(f"unit_loaded{i}") for i in range(G)]
        s_pc, s_dc, s_pw, s_dw = sem("pool_constants"), sem("dve_constants"), sem("weights_made"), sem("weights_kept")
        s_degd, s_dega, s_degs = sem("degree_half_dve"), sem("degree_half_act"), sem("degree_steps")
        s_degr = sem("degree_root")
        NODE = ("deg", "agg0", "agg1", "gat")
        s_ln, s_root, s_hturn, s_hT, s_proj, s_pkeep = (
            {p: sem(f"{p}_{what}") for p in NODE}
            for what in ("norm_steps", "norm_root", "h_turned", "hT_kept", "projected", "projection_kept"))
        s_pkeep_act = sem("agg1_projection_kept_act")
        s_alo_pool = {p: sem(f"{p}_unit_low_pool") for p in ("agg0", "agg1")}
        s_scale = {p: sem(f"{p}_scale_steps") for p in ("agg0", "agg1")}
        s_bnstat = sem("bn_statistics")
        s_bn, s_bnroot, s_bnnorm, s_bnturn = sem("bn_steps"), sem("bn_root"), sem("bn_normalised"), sem("bn_turned")
        s_ahi, s_alo = ({p: sem(f"{p}_unit_{what}") for p in ("agg0", "agg1")} for what in ("high", "low"))
        PASSES = ("agg0", "agg1", "gat", "edge", "norm", "out")
        s_mm = {p: sem(f"{p}_unit_multiplied") for p in PASSES}
        s_half, s_sum, s_turn = ({p: sem(f"{p}_{what}") for p in PASSES[:5]}
                                 for what in ("half_kept", "sum_kept", "sum_turned"))
        s_cut = {p: sem(f"{p}_turned_kept") for p in ("edge", "norm")}
        s_mask = {p: sem(f"{p}_masks") for p in ("edge", "norm")}
        s_e02, s_hall = sem("gat_exponentials"), sem("gat_hT_stored")
        s_gmax, s_grelu, s_gexp, s_gy = sem("gat_max"), sem("gat_relu"), sem("gat_exp"), sem("gat_weights")
        s_gmm = s_mm["gat"]
        s_gdd, s_gdp, s_gden = sem("gat_den_dve"), sem("gat_den_pool"), sem("gat_den_summed")
        s_fix = {p: sem(f"{p}_diagonal_cleared") for p in ("edge", "norm", "out")}
        s_ee, s_prep, s_ptop, s_vexp = sem("edge_steps"), sem("prep_steps"), sem("prep_top"), sem("prep_exp")
        s_flag = sem("flag_ready")
        s_ne, s_nexp, s_nturn, s_nrow = sem("norm_steps"), sem("norm_exp"), sem("norm_rows_turned"), sem("norm_rows_kept")
        s_clamp, s_exp, s_y, s_used = sem("out_clamped"), sem("out_exp"), sem("out_weights"), sem("out_tile_used")
        s_slow = sem("out_negative_steps")
        s_gg, s_ggk, s_rr, s_rrk = sem("guards_spread"), sem("guards_kept"), sem("dens_spread"), sem("dens_kept")
        s_nk, s_es, s_esk = sem("out_sums_kept"), sem("edge_support"), sem("edge_support_kept")
        s_gm, s_ga, s_gv = sem("gates_multiplied"), sem("gates_tanh"), sem("gates_steps")
        s_ot, s_res, s_store = sem("out_turned"), sem("out_result"), sem("out_stored")

        def hold(eng):
            eng.sem_inc(s_passed, 1)

        def loaded(p, c, g):
            if p == "out":
                return s_unit[g % RING_OUT], c * 32 + (16 * C * 5 + 16 * (g // RING_OUT + 1))
            return s_unit[g], c * 16 + (16 * C * PASSES.index(p) + 16)

        def ring_at(p, g, off=0, size=UNIT):
            slot = g % RING_OUT if p == "out" else g
            return slice(slot * UNIT + off, slot * UNIT + off + size)

        last_reader = {"agg0": s_mm["agg0"], "agg1": s_mm["agg1"], "gat": s_gy,
                       "edge": s_mask["edge"], "norm": s_mask["norm"], "out": s_mm["out"]}

        block = ctx.enter_context(nc.Block())

        @block.sync
        def _(sp):
            sp.dma_start(x[:, :].rearrange("p (t f) -> p t f", f=P),
                         x_d.rearrange("(t p) f -> p t f", p=P)).then_inc(s_xin, 16)
            for dst, src in ((wts, w_d), (cols, col_d), (rows, row_d), (gru, gru_d), (diag, diag_d)):
                sp.dma_start(dst[:, :], src).then_inc(s_const, 16)

            for s in range(4):
                sp.dma_start(ring[:, s * N:(s + 1) * N], rows_d[s * P:(s + 1) * P, :]).then_inc(s_rows[s], 16)
            with sp.Fori(1, C) as c:
                for s in range(4):
                    sp.wait_ge(s_degd, c * 4 + (s - 3))
                    sp.wait_ge(s_dega, c * 4 + (s - 3))
                    sp.dma_start(ring[:, s * N:(s + 1) * N], rows_d[at(c, W, s * P, P), :]).then_inc(s_rows[s], 16)

            def load(p, c, g):
                sp.dma_start(ring[:, ring_at(p, g)], cols_d[at(c, G * P, g * P, P), :]).then_inc(loaded(p, 0, g)[0], 16)

            before = None
            for p in PASSES:
                slots = RING_OUT if p == "out" else G
                for g in range(G):
                    if g >= slots:
                        sp.wait_ge(last_reader[p], g - slots + 1)
                    elif before is None:
                        sp.wait_ge(s_degd, T - 3 + g // 2)
                        sp.wait_ge(s_dega, T - 3 + g // 2)
                    else:
                        sp.wait_ge(last_reader[before], G * (C - 1) + g + 1)
                    load(p, 0, g)
                with sp.Fori(1, C) as c:
                    for g in range(G):
                        sp.wait_ge(last_reader[p], c * G + (g - slots + 1))
                        load(p, c, g)
                before = p

        @block.gpsimd
        def _(pool):
            pool.memset(ident[:, :], 0.0).then_inc(s_pc, 1)
            pool.memset(ones[:, :], 1.0).then_inc(s_pc, 1)
            pool.memset(grows[:, N:N + W], 0.0).then_inc(s_pc, 1)
            pool.wait_ge(s_pc, 3)
            pool.affine_select(out=ident[:, :], in_=ident[:, :], compare_op=ALU.not_equal, fill=1.0,
                               base=0, pattern=[[-1, P]], channel_multiplier=1).then_inc(s_pc, 1)

            for p in ("agg0", "agg1"):
                with pool.Fori(0, C) as c:
                    for g in POOL_UNITS:
                        pool.wait_ge(s_ahi[p], c * G + (g + 1))
                        pool.tensor_tensor(a_lo[:, ring_at(p, g)], ring[:, ring_at(p, g)],
                                           a_hi[:, (g % 4) * UNIT:(g % 4 + 1) * UNIT].bitcast(F32),
                                           ALU.subtract).then_inc(s_alo_pool[p], 1)

            def gat_body(c, first):
                if not first:
                    pool.wait_ge(s_gden, c)
                for g in range(G):
                    for q in range(1, Q):
                        m = g * Q + q
                        y = gunit(g)[:, q * W:(q + 1) * W]
                        pool.wait_ge(s_gy, c * G + (g + 1))
                        if m == 1:
                            hold(pool)
                            pool.tensor_copy(den_p, y).then_inc(s_gdp, 1)
                        else:
                            pool.wait_ge(s_gdp, c * (T - G) + (g * (Q - 1) + q - 1))
                            pool.tensor_tensor(den_p, den_p, y, ALU.add).then_inc(s_gdp, 1)
            over_chunks(pool, gat_body)

        @block.scalar
        def _(act):
            def root(p, c):
                act.wait_ge(s_ln[p], c * LN_STEPS[p] + LN_ROOT[p])
                act.activation(rstd[:, Q:2 * Q], rstd[:, 0:Q], ACT.Sqrt).then_inc(s_root[p], 1)

            def keep_hT(p, c, first, func):
                act.wait_ge(s_hturn[p], c + 1)
                if not first:
                    act.wait_ge(s_proj[p], c)
                elif p != "deg":
                    act.wait_ge(s_proj[NODE[NODE.index(p) - 1]], C)
                act.activation(hT[:, :], bank[3][:, :], func).then_inc(s_hT[p], 1)

            def keep_half(p, c, first, m=P):
                act.wait_ge(s_mm[p], c * G + G // 2)
                if not first:
                    act.wait_ge(s_sum[p], c)
                elif p != "agg0":
                    act.wait_ge(s_sum[PASSES[PASSES.index(p) - 1]], C)
                act.activation(half[0:m, :], bank[0][0:m, :], ACT.Copy).then_inc(s_half[p], 1)

            def deg_body(c, first):
                for s in range(4):
                    act.wait_ge(s_rows[s], c * 16 + 16)
                    if s or not first:
                        act.wait_ge(s_dega, c * 4 + s)
                    act.activation(work[:, 0:N // 2], ring[:, s * N + N // 2:(s + 1) * N], ACT.Copy,
                                   accum_out=degp[:, at(c, 2 * Q, 2 * s + 1, 1)]).then_inc(s_dega, 1)
                    if s == 0:
                        root("deg", c)
                    if s == 2:
                        keep_hT("deg", c, first, ACT.Relu)
            over_chunks(act, deg_body)
            act.wait_ge(s_degs, 3)
            act.activation(deg[:, 3 * T:5 * T], deg[:, T:3 * T], ACT.Sqrt).then_inc(s_degr, 1)

            def project_keep(p, c):
                act.wait_ge(s_proj[p], c + 1)
                if p == "agg0":
                    act.activation(reg3[:, at(c, W, 0, W)], bank[4][:, :], ACT.Identity,
                                   bias=cols[:, 0:1]).then_inc(s_pkeep[p], 1)
                else:
                    act.activation(reg3[:, at(c, W, 0, W)], bank[4][:, :], ACT.Copy)
                    act.activation(reg4[:, at(c, W, 0, W)], bank[5][:, :], ACT.Copy,
                                   scale=1 - SLOPE).then_inc(s_pkeep_act, 1)

            for p in ("agg0", "agg1"):
                def finish_hT(p, c):
                    act.wait_ge(s_hturn[p], c)
                    act.wait_ge(s_proj["deg" if p == "agg0" else "agg0"], C)
                    act.wait_ge(s_proj[p], c - 1)
                    act.activation(hT[:, :], bank[3][:, :], ACT.Relu).then_inc(s_hT[p], 1)

                def agg_body(c, before, two_before, p=p):
                    for g in range(G):
                        if before and g == 7:
                            root(p, c - 1)
                        if two_before and g == 2:
                            finish_hT(p, c - 1)
                        if two_before and g == 4:
                            project_keep(p, c - 2)
                        act.wait_ge(*loaded(p, c, g))
                        if g >= 4 or before:
                            act.wait_ge(s_mm[p], c * G + (g - 3))
                        elif p == "agg1":
                            act.wait_ge(s_mm["agg0"], G * C - 3 + g)
                        elif g == 0:
                            act.wait_ge(s_dega, T)
                        act.activation(a_hi[:, (g % 4) * UNIT:(g % 4 + 1) * UNIT],
                                       ring[:, ring_at(p, g)], ACT.Copy).then_inc(s_ahi[p], 1)
                    keep_half(p, c, not before)

                over_chunks_deep(act, agg_body)
                finish_hT(p, C - 1)
                project_keep(p, C - 2)
                root(p, C - 1)
                finish_hT(p, C)
                project_keep(p, C - 1)
                if p == "agg0":
                    act.wait_ge(s_bn, 2)
                    act.activation(bnmv[:, 3:4], bnmv[:, 2:3], ACT.Sqrt).then_inc(s_bnroot, 1)

            act.wait_ge(s_pkeep["agg1"], C)
            elr_v = elr[:, :].rearrange("p (t h) -> p h t", h=2)
            act.activation(el02[:, :], elr_v[:, 0, :], ACT.Exp, scale=SLOPE).then_inc(s_e02, 1)
            act.activation(er02[:, :], elr_v[:, 1, :], ACT.Copy, scale=SLOPE).then_inc(s_e02, 1)
            act.activation(er08[:, :], elr_v[:, 1, :], ACT.Copy, scale=1 - SLOPE).then_inc(s_e02, 1)
            act.wait_ge(s_pkeep_act, C)
            act.wait_ge(s_e02, 3)
            act.wait_ge(s_mm["agg1"], G * C)

            def store_hT(c):
                act.wait_ge(s_hturn["gat"], c)
                act.wait_ge(s_proj["agg1"], C)
                act.wait_ge(s_proj["gat"], c - 1)
                act.activation(hT[:, :], bank[3][:, :], ACT.Copy).then_inc(s_hT["gat"], 1)
                act.activation(reg2[:, at(c, W, -W, W)], bank[3][:, :], ACT.Copy).then_inc(s_hall, 1)

            def gat_body(c, before, two_before):
                for g in range(G):
                    if before and g == 6:
                        root("gat", c - 1)
                    if two_before and g == 1:
                        store_hT(c - 1)
                    if g >= GBUFS or before:
                        act.wait_ge(s_gmm, c * G + gat_user(g))
                        act.wait_ge(s_gdp, c * (T - G) + gat_user(g) * (Q - 1))
                        hold(act)
                    for q in (2, 3):
                        m = g * Q + q
                        act.activation(gunit(g)[:, q * W:(q + 1) * W], reg4[:, at(c, W, 0, W)], ACT.Relu,
                                       bias=er08[:, m:m + 1]).then_inc(s_grelu, 1)
                    act.wait_ge(s_gmax, c * G + (g + 1))
                    act.activation(gunit(g)[:, 0:2 * W], gunit(g)[:, 0:2 * W], ACT.Exp).then_inc(s_gexp, 1)
                    act.wait_ge(s_grelu, c * (2 * G) + 2 * (g + 1))
                    for q in (2, 3):
                        m, y = g * Q + q, gunit(g)[:, q * W:(q + 1) * W]
                        act.activation(y, y, ACT.Exp, bias=er02[:, m:m + 1]).then_inc(s_gexp, 1)
                    if g == 6:
                        keep_half("gat", c, not before)
            over_chunks_deep(act, gat_body)
            store_hT(C - 1)
            root("gat", C - 1)
            store_hT(C)

            def cut(p, c):
                act.wait_ge(s_turn[p], c + 1)
                if p == "edge":
                    act.activation(eraw[:, :], bank[2][:, 0:Q * ECOLS], ACT.Copy).then_inc(s_cut[p], 1)
                else:
                    act.activation(vcut, bank[2][:, 0:Q * VCOLS], ACT.Copy).then_inc(s_cut[p], 1)

            def edge_body(c, first):
                if not first:
                    if not isinstance(c, int):
                        act.wait_ge(s_ee, c * EDGE_STEPS - EDGE_STEPS)
                    cut("edge", c - 1)
                keep_half("edge", c, first, ECOLS)
            over_chunks(act, edge_body)
            act.wait_ge(s_ee, (C - 1) * EDGE_STEPS)
            cut("edge", C - 1)

            for sign in range(2):
                act.wait_ge(s_prep, PREP_HEAD + sign * PREP_SIGN + 2)
                act.activation(vtmp[1], vtmp[1], ACT.Exp).then_inc(s_vexp, 1)

            def guards(c):
                act.wait_ge(s_ne, c * NORM_STEPS + NORM_EXP)
                act.activation(gd[:, 5 * Q * HEADS:6 * Q * HEADS], gd[:, 4 * Q * HEADS:5 * Q * HEADS],
                               ACT.Exp).then_inc(s_nexp, 1)

            def guard_rows(c):
                act.wait_ge(s_nturn, c + 1)
                act.activation(grows[:, at(c, W, 0, W)], bank[3][0:SCORES, :], ACT.Copy).then_inc(s_nrow, 1)

            def norm_body(c, first):
                if not first:
                    act.wait_ge(s_ne, c * NORM_STEPS - NORM_STEPS)
                    cut("norm", c - 1)
                    guards(c - 1)
                keep_half("norm", c, first, VCOLS)
                if not first:
                    guard_rows(c - 1)
            act.wait_ge(s_prep, PREP_HEAD + 2 * PREP_SIGN)
            over_chunks(act, norm_body)
            act.wait_ge(s_ne, (C - 1) * NORM_STEPS)
            cut("norm", C - 1)
            guards(C - 1)
            guard_rows(C - 1)

            SPREAD = (4, 6, 7)

            def keep_guards(c):
                act.wait_ge(s_gg, c + 1)
                act.wait_ge(s_clamp, c * T)
                for k in range(HEADS):
                    last = act.activation(negg[:, k * W:(k + 1) * W], bank[SPREAD[k]][:, :], ACT.Copy)
                last.then_inc(s_ggk, 1)

            def keep_dens(c, first):
                act.wait_ge(s_rr, c + 1)
                if not first:
                    act.wait_ge(s_nk, c)
                for k in range(HEADS):
                    last = act.activation(rden[:, k * W:(k + 1) * W], bank[5 + k][:, :], ACT.Copy)
                last.then_inc(s_rrk, 1)

            def keep_edge_support(c):
                act.wait_ge(s_es, c)
                act.wait_ge(s_gm, c * 2 - 2)
                act.activation(esT, bank[4][:, :], ACT.Copy, scale=1.0 / HEADS).then_inc(s_esk, 1)

            def gates(c, cell):
                act.wait_ge(s_gm, c * 2 + (cell - 1))
                act.wait_ge(s_gv, c * CELL_STEPS + (cell * CELL_B - CELL_STEPS))
                act.activation(gr, bank[5][:, :], ACT.Tanh, bias=gb[:, 4 * cell:4 * cell + 1], scale=0.5)
                act.activation(gz, bank[6][:, :], ACT.Tanh, bias=gb[:, 4 * cell + 1:4 * cell + 2],
                               scale=0.5).then_inc(s_ga, 1)

            def candidate(c, cell):
                act.wait_ge(s_gv, c * CELL_STEPS + (cell * CELL_B - CELL_STEPS + CELL_A))
                act.activation(gn, gt, ACT.Tanh).then_inc(s_ga, 1)

            def store(c):
                act.wait_ge(s_res, c)
                act.dma_start(out_d.rearrange("(t p) f -> p t f", p=P)[:, at(c, Q, -Q, Q), :],
                              res.rearrange("p (t f) -> p t f", f=P)).then_inc(s_store, 16)

            def out_body(c, first):
                for g in range(G):
                    if not first:
                        if g == 2:
                            gates(c, 0)
                        if g == 3:
                            candidate(c, 0)
                            keep_edge_support(c)
                        if g == 5:
                            gates(c, 1)
                        if g == 6:
                            candidate(c, 1)
                        if g == 7:
                            store(c)
                    if g == 3:
                        keep_dens(c, first)
                    for t in range(g * Q, (g + 1) * Q):
                        if t == T - AHEAD:
                            keep_guards(c + 1)
                        act.wait_ge(s_clamp, c * T + (t + 1))
                        act.activation(tiles(t), tiles(t), ACT.Exp).then_inc(s_exp, 1)

            keep_guards(0)
            over_chunks(act, out_body)
            for cell in range(2):
                gates(C, cell)
                candidate(C, cell)
                if cell == 0:
                    keep_edge_support(C)
            store(C)
            act.wait_ge(s_store, 16 * C)

        @block.vector
        def _(dve):
            def spread(ap, n, axis=2):
                shape = [P, ap.shape[1]]
                shape.insert(axis, n)
                return ap.unsqueeze(axis).to_broadcast(shape)

            s = Steps(dve, s_dc, 2, 0)
            for b in range(WINDOWS):
                dve.memset(wconst[:, b:b + 1], STEP * b + LIFT)
                dve.memset(wconst[:, WINDOWS + b:WINDOWS + b + 1], float(WINDOWS - b))
            dve.wait_ge(s_pc, 4)
            dve.tensor_scalar(offdiag[:, :], ident[:, :], -1.0, 1.0, ALU.mult, ALU.add)
            s.inc(dve.tensor_copy(pick[:, :].rearrange("p (r m) -> p r m", r=SCORES),
                                  ident[0:SCORES, 0:SCORES].unsqueeze(2).to_broadcast([SCORES, SCORES, P])))
            dve.wait_ge(s_const, 16 * 5)
            for cell in range(2):
                bi, bh = 9 + 6 * cell, 12 + 6 * cell
                dve.tensor_tensor(gb[:, 4 * cell:4 * cell + 2], cols[:, bi:bi + 2], cols[:, bh:bh + 2], ALU.add)
                dve.tensor_copy(gb[:, 4 * cell + 2:4 * cell + 3], cols[:, bi + 2:bi + 3])
                last = dve.tensor_copy(gb[:, 4 * cell + 3:4 * cell + 4], cols[:, bh + 2:bh + 3])
            s.link(last)
            s.done()
            gb_v = gb[:, :].rearrange("p (c g) -> p c g", g=4)[:, :, 0:2]
            s = Steps(dve, s_dw, 2, 0)
            s.inc(dve.tensor_scalar(gb_v, gb_v, 0.5, None, ALU.mult))
            dve.wait_ge(s_pw, 1)
            dve.tensor_copy(wlr[:, :], bank[7][:, 0:2])
            dve.tensor_copy(wel[:, :], bank[7][:, 0:1].to_broadcast([P, P]))
            dve.tensor_copy(wa[:, :].rearrange("p (h k) -> p h k", h=2),
                            bank[7][:, 2:2 + SCORES].rearrange("p (k h) -> p h k", h=2))
            s.inc(dve.tensor_copy(b2all[:, :], bank[6][:, 0:P]))
            s.done()

            def per_tile(ap):
                return ap.rearrange("p (q f) -> p q f", q=Q)

            def norm_in(s, c):
                for q in range(Q):
                    last = dve.bn_stats(stats[:, q * 6:(q + 1) * 6], x[:, at(c, W, q * P, P)])
                s.link(last)
                hold(dve)
                for q in range(Q):
                    last = dve.bn_aggr(mv[:, q * 2:(q + 1) * 2], stats[:, q * 6:(q + 1) * 6])
                s.link(last)
                s.inc(dve.tensor_scalar(rstd[:, 0:Q], mv[:, 1:2 * Q:2], EPS, None, ALU.add))

            def norm_out(s, p, c, cc):
                dve.wait_ge(s_root[p], cc)
                s.link(dve.reciprocal(rstd[:, 2 * Q:3 * Q], rstd[:, Q:2 * Q]))
                for q in range(Q):
                    last = dve.tensor_scalar(hn[:, q * P:(q + 1) * P], x[:, at(c, W, q * P, P)],
                                             mv[:, 2 * q:2 * q + 1], rstd[:, 2 * Q + q:2 * Q + q + 1],
                                             ALU.subtract, ALU.mult)
                return last

            dve.wait_ge(s_xin, 16)

            def deg_body(c, first):
                s = Steps(dve, s_ln["deg"], LN_STEPS["deg"], c)
                for t in range(4):
                    if t == 0:
                        norm_in(s, c)
                    if t == 1:
                        if not first:
                            dve.wait_ge(s_hturn["deg"], c)
                        s.inc(norm_out(s, "deg", c, c + 1))
                        s.done()
                    dve.wait_ge(s_rows[t], c * 16 + 16)
                    dve.tensor_reduce(degp[:, at(c, 2 * Q, 2 * t, 1)], ring[:, t * N:t * N + N // 2],
                                      AX.X, ALU.add).then_inc(s_degd, 1)
                dve.wait_ge(s_proj["deg"], c + 1)
                dve.tensor_copy(reg3[:, at(c, W, 0, W)], bank[4][:, :]).then_inc(s_pkeep["deg"], 1)
            over_chunks(dve, deg_body)

            s = Steps(dve, s_degs, 5, 0)
            dve.wait_ge(s_degd, T)
            dve.wait_ge(s_dega, T)
            degp_v = degp[:, :].rearrange("p (t h) -> p h t", h=2)
            s.link(dve.tensor_tensor(deg[:, 0:T], degp_v[:, 0, :], degp_v[:, 1, :], ALU.add))
            s.link(dve.tensor_scalar(deg[:, 0:T], deg[:, 0:T], 1.0, None, ALU.add))
            dve.tensor_scalar(deg[:, 2 * T:3 * T], deg[:, 0:T], 1.0e-30, None, ALU.max)
            s.inc(dve.scalar_tensor_tensor(deg[:, T:2 * T], deg[:, 0:T], 0.0, deg[:, 0:T], ALU.is_equal, ALU.add))
            dve.wait_ge(s_degr, 1)
            s.link(dve.reciprocal(deg[:, 5 * T:7 * T], deg[:, 3 * T:5 * T]))
            dve.scalar_tensor_tensor(dinv0[:, :], deg[:, 0:T], 0.0, deg[:, 5 * T:6 * T], ALU.not_equal, ALU.mult)
            s.link(dve.scalar_tensor_tensor(dinv1[:, :], deg[:, 0:T], 0.0, deg[:, 6 * T:7 * T], ALU.is_gt, ALU.mult))
            s.done()

            def scale(p, g):
                s = Steps(dve, s_scale[p], 3, g)
                dinv = (dinv0 if p == "agg0" else dinv1)[:, g * Q:(g + 1) * Q]
                if p == "agg0":
                    src = reg3[:, g * W:(g + 1) * W]
                else:
                    dve.wait_ge(s_bnturn, g + 1)
                    src = bank[2][:, :]
                s.link(dve.tensor_tensor(per_tile(hn[:, :]), per_tile(src), spread(dinv, P), ALU.mult))
                s.link(dve.tensor_copy(s_hi[:, g * W:(g + 1) * W], hn[:, :]))
                s.link(dve.tensor_tensor(s_lo[:, g * W:(g + 1) * W], hn[:, :],
                                        s_hi[:, g * W:(g + 1) * W].bitcast(F32), ALU.subtract))
                s.done()

            def bn_norm(g):
                if g:
                    dve.wait_ge(s_bnturn, g)
                dve.tensor_scalar(outT[:, :], reg3[:, g * W:(g + 1) * W], bnmv[:, 0:1], bnmv[:, 5:6],
                                  ALU.subtract, ALU.mult).then_inc(s_bnnorm, 1)

            def take_sum(p, c, first, m=P):
                dve.wait_ge(s_mm[p], c * G)
                dve.wait_ge(s_half[p], c)
                if first:
                    if p == "agg1":
                        dve.wait_ge(s_bnturn, C)
                else:
                    dve.wait_ge(s_turn[p], c - 1)
                dve.tensor_tensor(outT[0:m, :], bank[1][0:m, :], half[0:m, :], ALU.add).then_inc(s_sum[p], 1)

            def agg_nodes_in(p, c, s):
                dinv = dinv0 if p == "agg0" else dinv1
                dve.wait_ge(s_turn[p], c)
                dve.wait_ge(s_hturn[p], c - 1)
                s.link(dve.tensor_tensor(hn[:, :], bank[2][:, :], s_hi[:, at(c, W, -W, W)].bitcast(F32), ALU.add))
                s.link(dve.tensor_tensor(hn[:, :], hn[:, :], s_lo[:, at(c, W, -W, W)].bitcast(F32), ALU.add))
                for q in range(Q):
                    xq = x[:, at(c, W, q * P - W, P)]
                    last = dve.scalar_tensor_tensor(xq, hn[:, q * P:(q + 1) * P], dinv[:, at(c, Q, q - Q, 1)],
                                                    xq, ALU.mult, ALU.add)
                s.link(last)
                norm_in(s, c - 1)

            def agg_project(p, c):
                if p == "agg0":
                    dve.wait_ge(s_pkeep[p], c)
                    dve.bn_stats(bnst[:, at(c, 6, -6, 6)], reg3[:, at(c, W, -W, W)]).then_inc(s_bnstat, 1)
                else:
                    dve.wait_ge(s_proj[p], c)
                    dve.tensor_copy(elr[:, at(c, 2 * Q, -2 * Q, 2 * Q)], bank[6][:, 0:2 * Q]).then_inc(s_pkeep[p], 1)

            for p in ("agg0", "agg1"):
                if p == "agg1":
                    s = Steps(dve, s_bn, 4, 0)
                    dve.wait_ge(s_bnstat, C)
                    s.link(dve.bn_aggr(bnmv[:, 0:2], bnst[:, :]))
                    s.inc(dve.tensor_scalar(bnmv[:, 2:3], bnmv[:, 1:2], float(N) / (N - 1), None, ALU.mult))
                    dve.wait_ge(s_bnroot, 1)
                    s.link(dve.tensor_scalar(bnmv[:, 4:5], bnmv[:, 3:4], 1.0e-6, None, ALU.add))
                    s.link(dve.reciprocal(bnmv[:, 5:6], bnmv[:, 4:5]))
                    s.done()
                    bn_norm(0)

                def agg_body(c, before, two_before, p=p):
                    s = Steps(dve, s_ln[p], LN_STEPS[p], c - 1)
                    for g in range(G):
                        if not before:
                            if p == "agg1" and g + 1 < G:
                                bn_norm(g + 1)
                            scale(p, g)
                        if before and g == 2:
                            take_sum(p, c, isinstance(c, int) and c == 1)
                        if before and g == 4:
                            agg_nodes_in(p, c, s)
                        if two_before and g == 5:
                            agg_project(p, c - 1)
                        if before and g == 7:
                            s.inc(norm_out(s, p, c - 1, c))
                            s.done()
                        if g in DVE_UNITS:
                            dve.wait_ge(s_ahi[p], c * G + (g + 1))
                            dve.tensor_tensor(a_lo[:, ring_at(p, g)], ring[:, ring_at(p, g)],
                                              a_hi[:, (g % 4) * UNIT:(g % 4 + 1) * UNIT].bitcast(F32),
                                              ALU.subtract).then_inc(s_alo[p], 1)
                over_chunks_deep(dve, agg_body)
                agg_project(p, C - 1)
                take_sum(p, C, False)
                s = Steps(dve, s_ln[p], LN_STEPS[p], C - 1)
                agg_nodes_in(p, C, s)
                s.inc(norm_out(s, p, C - 1, C))
                s.done()
                agg_project(p, C)

            dve.wait_ge(s_e02, 3)
            dve.wait_ge(s_pkeep_act, C)
            dve.wait_ge(s_mm["agg1"], G * C)
            spv, smv = (a.rearrange("p (t e) -> p t e", e=ECOLS) for a in (sp_all, sm_all))
            dve.memset(spv[:, :, ECOLS - 1:ECOLS], 0.0)
            dve.memset(smv[:, :, ECOLS - 1:ECOLS], 1.0)

            def gat_nodes_in(c, s):
                e = el02[:, at(c, Q, -Q, Q)]
                dve.wait_ge(s_gden, c)
                dve.wait_ge(s_turn["gat"], c)
                s.link(dve.tensor_tensor(den[:, 0:Q], bank[7][:, 0:Q], e, ALU.mult))
                s.link(dve.tensor_scalar(den[:, Q:2 * Q], den[:, 0:Q], 1.0e-12, None, ALU.max))
                s.link(dve.reciprocal(den[:, 2 * Q:3 * Q], den[:, Q:2 * Q]))
                s.link(dve.tensor_tensor(den[:, 3 * Q:4 * Q], den[:, 2 * Q:3 * Q], e, ALU.mult))
                for q in range(Q):
                    xq = x[:, at(c, W, q * P - W, P)]
                    last = dve.scalar_tensor_tensor(xq, bank[2][:, q * P:(q + 1) * P],
                                                    den[:, 3 * Q + q:3 * Q + q + 1], xq, ALU.mult, ALU.add)
                s.link(last)
                xc = per_tile(x[:, at(c, W, -W, W)])
                s.link(dve.tensor_tensor(xc, xc, spread(b2all[:, :], Q, 1), ALU.add))
                norm_in(s, c - 1)

            def gat_nodes_out(c, s):
                dve.wait_ge(s_hturn["gat"], c - 1)
                s.link(norm_out(s, "gat", c - 1, c))
                s.link(dve.tensor_scalar(hn[:, :], hn[:, :], 0.0, None, ALU.max))
                s.inc(dve.tensor_copy(reg1[:, at(c, W, -W, W)], hn[:, :]))
                s.done()

            def gat_project(c):
                s = Steps(dve, s_pkeep["gat"], U_STEPS, c - 1)
                HS = Q * SCORES
                u, r = ucut[:, 0:HS], ucut[:, HS:2 * HS]
                uv, rv = (a.rearrange("p (t e) -> p t e", e=SCORES) for a in (u, r))
                spc, smc = (a[:, at(c, Q * ECOLS, -Q * ECOLS, Q * ECOLS)].rearrange("p (t e) -> p t e", e=ECOLS)
                            for a in (sp_all, sm_all))
                dve.wait_ge(s_proj["gat"], c)
                s.link(dve.tensor_copy(u, bank[4][:, 0:HS]))
                s.link(dve.tensor_copy(spc[:, :, 0:SCORES], uv))
                s.link(dve.tensor_tensor(rv, uv, spc[:, :, 0:SCORES], ALU.subtract))
                s.link(dve.tensor_copy(spc[:, :, SCORES:2 * SCORES], rv))
                s.link(dve.tensor_tensor(uv, rv, spc[:, :, SCORES:2 * SCORES], ALU.subtract))
                s.link(dve.tensor_copy(spc[:, :, 2 * SCORES:3 * SCORES], uv))
                for part in range(3):
                    a = part * SCORES
                    dve.tensor_copy(smc[:, :, a:a + HEADS], spc[:, :, a + HEADS:a + SCORES])
                    last = dve.tensor_copy(smc[:, :, a + HEADS:a + SCORES], spc[:, :, a:a + HEADS])
                s.inc(last)
                s.done()

            def gat_max(c, g, before):
                if g >= GBUFS or before:
                    dve.wait_ge(s_gmm, c * G + gat_user(g))
                    dve.wait_ge(s_gdp, c * (T - G) + gat_user(g) * (Q - 1))
                    dve.wait_ge(s_gdd, c * G + gat_user(g))
                for q in (0, 1):
                    m = g * Q + q
                    last = dve.tensor_scalar(gunit(g)[:, q * W:(q + 1) * W], reg4[:, at(c, W, 0, W)],
                                             elr[:, 2 * m + 1:2 * m + 2], er02[:, m:m + 1], ALU.add, ALU.max)
                last.then_inc(s_gmax, 1)

            def gat_body(c, before, two_before):
                s = Steps(dve, s_ln["gat"], LN_STEPS["gat"], c - 1)
                gat_max(c, 0, before)
                for g in range(G):
                    if g + 1 < G:
                        gat_max(c, g + 1, before)
                    if before and g == 1:
                        take_sum("gat", c, False)
                    dve.wait_ge(*loaded("gat", c, g))
                    dve.wait_ge(s_gexp, c * (3 * G) + 3 * (g + 1))
                    dve.scalar_tensor_tensor(gunit(g), ring[:, ring_at("gat", g)], 0.0, gunit(g),
                                             ALU.not_equal, ALU.mult).then_inc(s_gy, 1)
                    if before and g == 0:
                        dve.wait_ge(s_gden, c)
                    dve.wait_ge(s_gy, c * G + (g + 1))
                    y = gunit(g)[:, 0:W]
                    if g == 0:
                        dve.tensor_copy(den_v, y).then_inc(s_gdd, 1)
                    else:
                        dve.wait_ge(s_gdd, c * G + g)
                        dve.tensor_tensor(den_v, den_v, y, ALU.add).then_inc(s_gdd, 1)
                    if before and g == 3:
                        gat_nodes_in(c, s)
                    if before and g == 5:
                        gat_nodes_out(c, s)
                    if two_before and g == 2:
                        gat_project(c - 1)
            over_chunks_deep(dve, gat_body)
            gat_project(C - 1)
            take_sum("gat", C, False)
            s = Steps(dve, s_ln["gat"], LN_STEPS["gat"], C - 1)
            gat_nodes_in(C, s)
            gat_nodes_out(C, s)
            gat_project(C)

            def clear_diagonal(p, c, g):
                def clear():
                    for q in range(Q):
                        z = ring[:, ring_at(p, g, q * W + q * P, P)]
                        last = dve.tensor_tensor(z, z, offdiag[:, :], ALU.mult)
                    last.then_inc(s_fix[p], 1)
                    dve.wait_ge(s_fix[p], g + 1)
                if isinstance(c, int):
                    if c == g:
                        clear()
                else:
                    hold(dve)
                    with dve.If(c == g):
                        clear()

            def masks(p, c, g, first):
                dve.wait_ge(*loaded(p, c, g))
                clear_diagonal(p, c, g)
                if g >= 2 or not first:
                    dve.wait_ge(s_mm[p], c * G + (g - 1))
                elif p == "edge":
                    dve.wait_ge(s_gdp, (T - G) * C)
                    dve.wait_ge(s_gmm, G * C)
                    dve.wait_ge(s_gden, C)
                src, dst = ring[:, ring_at(p, g)], slice((g % 2) * UNIT, (g % 2 + 1) * UNIT)
                dve.tensor_scalar(pmask[:, dst], src, 0.0, None, ALU.is_gt)
                dve.tensor_scalar(mmask[:, dst], src, 0.0, None, ALU.is_lt).then_inc(s_mask[p], 1)

            def edge_nodes(c):
                s = Steps(dve, s_ee, EDGE_STEPS, c - 1)
                dve.wait_ge(s_cut["edge"], c)
                ev = eraw[:, :].rearrange("p (t e) -> p t e", e=ECOLS)
                es = esum[:, :].rearrange("p (t e) -> p t e", e=SCORES)
                s.link(dve.tensor_tensor(es, ev[:, :, 2 * SCORES:3 * SCORES], ev[:, :, SCORES:2 * SCORES], ALU.add))
                s.link(dve.tensor_tensor(es, es, ev[:, :, 0:SCORES], ALU.add))
                ec = e6[:, at(c, Q * SCORES, -Q * SCORES, Q * SCORES)]
                s.link(dve.scalar_tensor_tensor(ec, esum[:, :], SLOPE, esum[:, :], ALU.mult, ALU.max))
                ec = ec.rearrange("p (t e) -> p t e", e=SCORES)
                dec = d_e[:, at(c, Q * HEADS, -Q * HEADS, Q * HEADS)].rearrange("p (t e) -> p t e", e=HEADS)
                dve.tensor_tensor(dec, ec[:, :, HEADS:SCORES], ec[:, :, 0:HEADS], ALU.subtract)
                s.inc(dve.tensor_copy(cnt[:, at(c, Q, -Q, Q)].unsqueeze(2), ev[:, :, ECOLS - 1:ECOLS]))
                s.done()

            def edge_body(c, first):
                for g in range(G):
                    masks("edge", c, g, first)
                    if not first and g == 1:
                        take_sum("edge", c, False, ECOLS)
                    if not first and g == 5:
                        edge_nodes(c)
            over_chunks(dve, edge_body)
            take_sum("edge", C, False, ECOLS)
            edge_nodes(C)

            s = Steps(dve, s_prep, PREP_HEAD + 2 * PREP_SIGN, 0)
            dve.wait_ge(s_ee, C * EDGE_STEPS)
            dve.tensor_reduce(top[:, 0:HEADS], e6[:, :].rearrange("p (t h k) -> p k t h", h=2, k=HEADS),
                              AX.XY, ALU.max)
            s.inc(dve.tensor_reduce(top[:, HEADS:HEADS + 1], cnt[:, :], AX.X, ALU.max))
            dve.wait_ge(s_ptop, 1)
            H4 = HEADS + 1
            s.link(dve.tensor_reduce(top[0:H4, 4:5], bank[2][0:H4, 0:P], AX.X, ALU.max))
            s.inc(dve.tensor_scalar(top[0:H4, 8:8 + H4], ident[0:H4, 0:H4], top[0:H4, 4:5], None, ALU.mult))
            dve.wait_ge(s_ptop, 2)
            dve.tensor_scalar(flag[0:1, 0:1], bank[3][0:1, HEADS:H4], 0.0, None, ALU.is_gt).then_inc(s_flag, 1)
            s.link(dve.tensor_scalar(top[:, 12:12 + HEADS], bank[3][:, 0:HEADS], ROUND, None, ALU.add))
            s.link(dve.tensor_scalar(c0[:, 0:HEADS], top[:, 12:12 + HEADS], ROUND, 1.0, ALU.subtract, ALU.add))
            s.link(dve.tensor_scalar(c0[:, HEADS:2 * HEADS], c0[:, 0:HEADS], -1.0, None, ALU.mult))
            s.link(dve.tensor_scalar(c0[:, 2 * HEADS:3 * HEADS], c0[:, 0:HEADS], -(STEP * WINDOWS + LIFT), None, ALU.add))
            for k in range(HEADS):
                last = dve.tensor_scalar(shift[:, k * WINDOWS:(k + 1) * WINDOWS], wconst[:, 0:WINDOWS],
                                         c0[:, HEADS + k:HEADS + k + 1], None, ALU.add)
            s.link(last)
            dve.wait_ge(s_mm["edge"], G * C)
            dve.wait_ge(s_gmm, G * C)
            KW = HEADS * WINDOWS
            s.link(dve.memset(top[:, 16:17], 0.0))
            for sign, v in ((0, vp), (1, vm)):
                e_v = e6[:, :].rearrange("p (t h k) -> p t h k", h=2, k=HEADS)
                arg, capped, rest = (a.rearrange("p (t v) -> p t v", v=KW) for a in vtmp)
                parts = [v.rearrange("p (t v) -> p t v", v=VCOLS)[:, :, i * KW:(i + 1) * KW] for i in range(3)]
                for k in range(HEADS):
                    last = dve.tensor_tensor(arg[:, :, k * WINDOWS:(k + 1) * WINDOWS],
                                             e_v[:, :, sign, k:k + 1].to_broadcast([P, T, WINDOWS]),
                                             shift[:, k * WINDOWS:(k + 1) * WINDOWS].unsqueeze(1)
                                             .to_broadcast([P, T, WINDOWS]), ALU.add)
                s.link(last)
                s.inc(dve.tensor_scalar(vtmp[1], vtmp[0], LIFT, None, ALU.min))
                dve.wait_ge(s_vexp, sign + 1)
                s.link(dve.scalar_tensor_tensor(vtmp[2], vtmp[0], LIFT, vtmp[1], ALU.is_le, ALU.mult))
                s.link(dve.tensor_copy(parts[0], rest))
                s.link(dve.tensor_tensor(rest, rest, parts[0], ALU.subtract))
                s.link(dve.tensor_copy(parts[1], rest))
                s.link(dve.tensor_tensor(rest, rest, parts[1], ALU.subtract))
                s.link(dve.tensor_copy(parts[2], rest))
            s.done()

            def norm_nodes_in(c, s):
                def g_at(i):
                    return gd[:, i * Q * HEADS:(i + 1) * Q * HEADS]

                def win(a):
                    return a.rearrange("p (n b) -> p n b", b=WINDOWS)
                dve.wait_ge(s_cut["norm"], c)
                vv = vcut.rearrange("p (t v) -> p t v", v=VCOLS)
                dv = dsum.rearrange("p (t v) -> p t v", v=KW)
                s.link(dve.tensor_tensor(dv, vv[:, :, 2 * KW:3 * KW], vv[:, :, KW:2 * KW], ALU.add))
                s.link(dve.tensor_tensor(dv, dv, vv[:, :, 0:KW], ALU.add))
                s.link(dve.tensor_scalar(dok, dsum, WINDOW_MIN, None, ALU.is_ge))
                s.link(dve.tensor_tensor(win(dwin), win(dok), spread(wconst[:, WINDOWS:2 * WINDOWS], Q * HEADS, 1), ALU.mult))
                s.link(dve.tensor_reduce(g_at(0), win(dwin), AX.X, ALU.max))
                s.link(dve.tensor_tensor(win(dsel), win(dwin), spread(g_at(0), WINDOWS), ALU.is_equal))
                s.link(dve.tensor_tensor(dsel, dsel, dok, ALU.mult))
                s.link(dve.tensor_tensor(dsel, dsel, dsum, ALU.mult))
                s.link(dve.tensor_reduce(g_at(1), win(dsel), AX.X, ALU.add))
                s.link(dve.tensor_scalar(g_at(2), g_at(0), STEP, None, ALU.mult))
                g2 = g_at(2).rearrange("p (t k) -> p t k", k=HEADS)
                s.link(dve.tensor_tensor(g2, g2, spread(c0[:, 2 * HEADS:3 * HEADS], Q, 1), ALU.add))
                s.link(dve.tensor_scalar(g_at(3), g_at(1).bitcast(I32), LN2 / 2 ** 23, 0.1 - 127 * LN2,
                                         ALU.mult, ALU.add))
                s.link(dve.tensor_tensor(g_at(6), g_at(2), g_at(3), ALU.add))
                s.inc(dve.tensor_tensor(g_at(4), g_at(2), g_at(6), ALU.subtract))

            def norm_nodes_out(c, s):
                def g_at(i):
                    return gd[:, i * Q * HEADS:(i + 1) * Q * HEADS]
                dve.wait_ge(s_nexp, c)
                s.link(dve.tensor_tensor(g_at(0), g_at(1), g_at(5), ALU.mult))
                s.link(dve.tensor_scalar(g_at(0), g_at(0), 1.0e-30, None, ALU.max))
                dve.wait_ge(s_nturn, c - 1)
                nv = nr[:, :].rearrange("p (t e) -> p t e", e=SCORES)
                dve.tensor_scalar(nv[:, :, 0:HEADS], g_at(6).rearrange("p (t k) -> p t k", k=HEADS),
                                  -1.0, None, ALU.mult)
                s.inc(dve.reciprocal(nv[:, :, HEADS:SCORES], g_at(0).rearrange("p (t k) -> p t k", k=HEADS)))
                s.done()

            def norm_body(c, first):
                s = Steps(dve, s_ne, NORM_STEPS, c - 1)
                for g in range(G):
                    masks("norm", c, g, first)
                    if not first and g == 1:
                        take_sum("norm", c, False, VCOLS)
                    if not first and g == 3:
                        norm_nodes_in(c, s)
                    if not first and g == 5:
                        norm_nodes_out(c, s)
            over_chunks(dve, norm_body)
            take_sum("norm", C, False, VCOLS)
            s = Steps(dve, s_ne, NORM_STEPS, C - 1)
            norm_nodes_in(C, s)
            norm_nodes_out(C, s)

            negative = dve.value_load(flag[0:1, 0:1], min_val=0, max_val=1)

            def take_chunk(c):
                dve.wait_ge(s_mm["out"], c * G)
                dve.wait_ge(s_rrk, c)
                dve.wait_ge(s_es, c - 1)
                dve.wait_ge(s_gm, c * 2 - 2)
                dve.tensor_copy(nsT, bank[0][:, :])
                for k in range(HEADS):
                    last = dve.tensor_tensor(nk[:, k * W:(k + 1) * W], bank[1 + k][:, :],
                                             rden[:, k * W:(k + 1) * W], ALU.mult)
                last.then_inc(s_nk, 1)

            def cell_in(c, cell, s):
                dve.wait_ge(s_ga, c * 4 + (2 * cell - 3))
                s.link(dve.tensor_scalar(gr, gr, 0.5, 0.5, ALU.mult, ALU.add))
                s.link(dve.scalar_tensor_tensor(gt, bank[7][:, :], gb[:, 4 * cell + 3:4 * cell + 4], gr,
                                                ALU.add, ALU.mult))
                s.inc(dve.scalar_tensor_tensor(gt, bank[4][:, :], gb[:, 4 * cell + 2:4 * cell + 3], gt,
                                               ALU.add, ALU.add))

            def cell_out_steps(c, cell, s):
                dve.wait_ge(s_ga, c * 4 + (2 * cell - 2))
                s.link(dve.tensor_tensor(gr, reg2[:, at(c, W, -W, W)], gn, ALU.subtract))
                s.link(dve.scalar_tensor_tensor(gr, gz, 1.0, gr, ALU.add, ALU.mult))
                if cell == 0:
                    s.link(dve.scalar_tensor_tensor(cell_out, gr, 0.5, gn, ALU.mult, ALU.add))
                else:
                    dve.wait_ge(s_ot, c - 1)
                    s.link(dve.scalar_tensor_tensor(cells, gr, 0.5, gn, ALU.mult, ALU.add))
                    s.inc(dve.tensor_tensor(cells, cells, cell_out, ALU.add))
                    s.done()

            def result(c):
                dve.wait_ge(s_ot, c)
                dve.wait_ge(s_store, c * 16 - 16)
                for q in range(Q):
                    last = dve.scalar_tensor_tensor(res[:, q * P:(q + 1) * P], bank[5][:, q * P:(q + 1) * P],
                                                    diag[:, at(c, Q, q - Q, 1)], x[:, at(c, W, q * P - W, P)],
                                                    ALU.mult, ALU.add)
                last.then_inc(s_res, 1)

            def exponents(c, t, first, negatives):
                if t >= GROUPS or not first:
                    dve.wait_ge(s_used, c * T + (t + 1 - GROUPS))
                s = Steps(dve, s_slow, SLOW_STEPS, c * T + t)
                for k in range(HEADS):
                    arg = negg[:, k * W:(k + 1) * W]
                    if negatives:
                        if k == 0:
                            dve.wait_ge(*loaded("out", c, t // Q))
                            if t or not first:
                                dve.wait_ge(s_clamp, c * T + t)
                            s.link(dve.tensor_scalar(nmask, ring[:, ring_at("out", t // Q, (t % Q) * W, W)],
                                                        0.0, None, ALU.is_lt))
                        s.link(dve.scalar_tensor_tensor(slow, nmask, d_e[:, t * HEADS + k:t * HEADS + k + 1],
                                                           arg, ALU.mult, ALU.add))
                        arg = slow
                    last = dve.tensor_scalar(tiles(t)[:, k * W:(k + 1) * W], arg,
                                             e6[:, t * SCORES + k:t * SCORES + k + 1], 0.0, ALU.add, ALU.min)
                    if negatives and k < HEADS - 1:
                        s.link(last)
                last.then_inc(s_clamp, 1)

            def out_body(c, first, negatives):
                if not first:
                    s = Steps(dve, s_gv, CELL_STEPS, c - 1)
                dve.wait_ge(s_ggk, c + 1)
                for t in range(AHEAD):
                    exponents(c, t, first, negatives)
                for t in range(T):
                    if t + AHEAD < T:
                        exponents(c, t + AHEAD, first, negatives)
                    g, q = t // Q, t % Q
                    if q == 0:
                        dve.wait_ge(*loaded("out", c, g))
                        clear_diagonal("out", c, g)
                    dve.wait_ge(s_exp, c * T + (t + 1))
                    tv = tiles(t).rearrange("p (k i) -> p k i", k=HEADS)
                    dve.tensor_tensor(tv, tv, spread(ring[:, ring_at("out", g, q * W, W)], HEADS, 1),
                                      ALU.mult).then_inc(s_y, 1)
                    if not first:
                        if t == 0:
                            take_chunk(c)
                        if t == 7:
                            cell_in(c, 0, s)
                        if t == 11:
                            cell_out_steps(c, 0, s)
                        if t == 19:
                            cell_in(c, 1, s)
                        if t == 23:
                            cell_out_steps(c, 1, s)
                        if t == 27:
                            result(c)

            with dve.If(negative == 0):
                over_chunks(dve, lambda c, first: out_body(c, first, False))
            with dve.Else():
                over_chunks(dve, lambda c, first: out_body(c, first, True))
            take_chunk(C)
            s = Steps(dve, s_gv, CELL_STEPS, C - 1)
            for cell in range(2):
                cell_in(C, cell, s)
                cell_out_steps(C, cell, s)
            result(C)

        @block.tensor
        def _(pe):
            def turn(dst, src, m=P):
                for q in range(Q):
                    last = pe.transpose(dst[:, q * m:(q + 1) * m], src[0:m, q * P:(q + 1) * P], ident[0:m, 0:m])
                return last

            pe.wait_ge(s_const, 16 * 5)
            pe.wait_ge(s_pc, 4)
            pe.matmul(bank[6][:, 0:P], ones[0:1, :], rows[0:1, P:2 * P], start=True, stop=True)
            pe.matmul(bank[7][:, 0:2], w2t, cols[:, 1:3], start=True, stop=True)
            for k in range(HEADS):
                last = pe.matmul(bank[7][:, 2 + 2 * k:4 + 2 * k], gat_wt[k], cols[:, 3 + 2 * k:5 + 2 * k],
                                 start=True, stop=True)
            last.then_inc(s_pw, 1)

            def turn_h(p, c):
                pe.wait_ge(s_ln[p], c * LN_STEPS[p])
                if not (isinstance(c, int) and c == 1):
                    pe.wait_ge(s_hT[p], c - 1)
                elif p != "deg":
                    pe.wait_ge(s_hT[NODE[NODE.index(p) - 1]], C)
                if p == "gat":
                    pe.wait_ge(s_hall, c - 1) if not (isinstance(c, int) and c == 1) else None
                turn(bank[3], hn).then_inc(s_hturn[p], 1)

            def project(p, c):
                pe.wait_ge(s_hT[p], c)
                if p == "deg":
                    if not (isinstance(c, int) and c == 1):
                        pe.wait_ge(s_pkeep[p], c - 1)
                    for q in range(Q):
                        o = bank[4][:, q * P:(q + 1) * P]
                        pe.matmul(o, ones[0:1, :], rows[0:1, 0:P], start=True, stop=False)
                        last = pe.matmul(o, hT[:, q * P:(q + 1) * P], w0t, start=False, stop=True)
                elif p == "agg0":
                    pe.wait_ge(s_pkeep["deg"], C)
                    pe.wait_ge(s_pkeep[p], c - 1)
                    last = pe.matmul(bank[4][:, :], w1t, hT[:, :], start=True, stop=True)
                elif p == "agg1":
                    pe.wait_ge(s_pkeep["agg0"], C)
                    pe.wait_ge(s_dw, 2)
                    pe.wait_ge(s_pkeep[p], c - 1)
                    pe.wait_ge(s_pkeep_act, c - 1)
                    pe.matmul(bank[5][:, :], wel[:, :], hT[:, :], start=True, stop=True)
                    for q in range(Q):
                        pe.matmul(bank[6][:, 2 * q:2 * q + 2], hT[:, q * P:(q + 1) * P], wlr[:, :],
                                  start=True, stop=True)
                    for q in range(Q):
                        last = pe.matmul(bank[4][:, q * P:(q + 1) * P], hT[:, q * P:(q + 1) * P], w2,
                                         start=True, stop=True)
                else:
                    pe.wait_ge(s_pkeep_act, C)
                    pe.wait_ge(s_pkeep[p], (c - 1) * U_STEPS)
                    for q in range(Q):
                        last = pe.matmul(bank[4][:, q * SCORES:(q + 1) * SCORES], hT[:, q * P:(q + 1) * P],
                                         wa[:, :], start=True, stop=True)
                last.then_inc(s_proj[p], 1)

            def deg_body(c, first):
                turn_h("deg", c + 1)
                project("deg", c + 1)
            pe.wait_ge(s_ln["deg"], LN_STEPS["deg"])
            turn(bank[3], hn).then_inc(s_hturn["deg"], 1)
            project("deg", 1)
            with pe.Fori(2, C + 1) as c:
                turn_h("deg", c)
                project("deg", c)

            def turn_sum(p, c, m=P):
                pe.wait_ge(s_sum[p], c)
                if p in ("edge", "norm"):
                    if not (isinstance(c, int) and c == 1):
                        pe.wait_ge(s_cut[p], c - 1)
                    else:
                        pe.wait_ge(s_ln["gat"], C * LN_STEPS["gat"])
                else:
                    pe.wait_ge(s_ln[p], (c - 1) * LN_STEPS[p])
                hold(pe)
                turn(bank[2], outT, m).then_inc(s_turn[p], 1)

            def accumulator(p, c, first, g):
                if g == 0:
                    if not first:
                        pe.wait_ge(s_half[p], c)
                    elif p != "agg0":
                        pe.wait_ge(s_half[PASSES[PASSES.index(p) - 1]], C)
                if g == G // 2:
                    if not first:
                        pe.wait_ge(s_sum[p], c)
                    elif p != "agg0":
                        pe.wait_ge(s_sum[PASSES[PASSES.index(p) - 1]], C)
                return bank[g // (G // 2)]

            def limits(g, q):
                return (g % (G // 2) == 0 and q == 0), (g % (G // 2) == G // 2 - 1 and q == Q - 1)

            for p in ("agg0", "agg1"):
                def turn_bn(g):
                    pe.wait_ge(s_bnnorm, g + 1)
                    if g:
                        pe.wait_ge(s_scale["agg1"], 3 * (g - 1) + 1)
                    else:
                        pe.wait_ge(s_ln["agg0"], C * LN_STEPS["agg0"])
                    turn(bank[2], outT).then_inc(s_bnturn, 1)

                def agg_body(c, before, two_before, p=p):
                    for g in range(G):
                        acc = accumulator(p, c, not before, g)
                        if not before:
                            if p == "agg1" and g == 0:
                                turn_bn(0)
                            if p == "agg1" and g + 1 < G:
                                turn_bn(g + 1)
                            pe.wait_ge(s_scale[p], 3 * (g + 1))
                        if g in DVE_UNITS:
                            pe.wait_ge(s_alo[p], c * len(DVE_UNITS) + (DVE_UNITS.index(g) + 1))
                        else:
                            pe.wait_ge(s_alo_pool[p], c * len(POOL_UNITS) + (POOL_UNITS.index(g) + 1))
                        for q in range(Q):
                            t = g * Q + q
                            begin, end = limits(g, q)
                            hi = a_hi[:, (g % 4) * UNIT + q * W:(g % 4) * UNIT + (q + 1) * W]
                            lo = a_lo[:, ring_at(p, g, q * W, W)]
                            sh, sl = s_hi[:, t * P:(t + 1) * P], s_lo[:, t * P:(t + 1) * P]
                            pe.matmul(acc[:, :], sh, hi, start=begin, stop=False)
                            pe.matmul(acc[:, :], sh, lo, start=False, stop=False)
                            last = pe.matmul(acc[:, :], sl, hi, start=False, stop=end)
                        last.then_inc(s_mm[p], 1)
                        if two_before and g == 0:
                            project(p, c - 1)
                        if before and g == 1:
                            turn_sum(p, c)
                        if before and g == 6:
                            turn_h(p, c)
                over_chunks_deep(pe, agg_body)
                project(p, C - 1)
                turn_sum(p, C)
                turn_h(p, C)
                project(p, C)

            pe.wait_ge(s_pkeep_act, C)

            def gat_body(c, before, two_before):
                for g in range(G):
                    acc = accumulator("gat", c, not before, g)
                    pe.wait_ge(s_gy, c * G + (g + 1))
                    for q in range(Q):
                        m = g * Q + q
                        begin, end = limits(g, q)
                        last = pe.matmul(acc[:, :], reg3[:, m * P:(m + 1) * P],
                                         gunit(g)[:, q * W:(q + 1) * W], start=begin, stop=end)
                    last.then_inc(s_gmm, 1)
                    if two_before and g == 1:
                        project("gat", c - 1)
                    if before and g == 1:
                        turn_sum("gat", c)
                    if before and g == 5:
                        turn_h("gat", c)
                pe.wait_ge(s_gdd, c * G + G)
                pe.wait_ge(s_gdp, c * (T - G) + (T - G))
                if before:
                    pe.wait_ge(s_ln["gat"], c * LN_STEPS["gat"])
                for q in range(Q):
                    o = bank[7][:, q:q + 1]
                    pe.matmul(o, den_v[:, q * P:(q + 1) * P], ones[:, 0:1], start=True, stop=False)
                    last = pe.matmul(o, den_p[:, q * P:(q + 1) * P], ones[:, 0:1], start=False, stop=True)
                last.then_inc(s_gden, 1)
            over_chunks_deep(pe, gat_body)
            project("gat", C - 1)
            turn_sum("gat", C)
            turn_h("gat", C)
            project("gat", C)

            def masked(p, m, plus, minus, extra):
                def body(c, first):
                    for g in range(G):
                        acc = accumulator(p, c, first, g)
                        pe.wait_ge(s_mask[p], c * G + (g + 1))
                        for q in range(Q):
                            t = g * Q + q
                            begin, end = limits(g, q)
                            o = (g % 2) * UNIT + q * W
                            pe.matmul(acc[0:m, :], plus[:, t * m:(t + 1) * m], pmask[:, o:o + W],
                                      start=begin, stop=False)
                            last = pe.matmul(acc[0:m, :], minus[:, t * m:(t + 1) * m], mmask[:, o:o + W],
                                             start=False, stop=end)
                        last.then_inc(s_mm[p], 1)
                        if not first:
                            if g == 1:
                                turn_sum(p, c, m)
                            extra(c, g)
                return body

            pe.wait_ge(s_pkeep["gat"], C * U_STEPS)
            over_chunks(pe, masked("edge", ECOLS, sp_all, sm_all, lambda c, g: None))
            turn_sum("edge", C, ECOLS)

            pe.wait_ge(s_prep, 1)
            pe.wait_ge(s_cut["edge"], C)
            pe.transpose(bank[2][0:HEADS + 1, 0:P], top[:, 0:HEADS + 1], ident[:, :]).then_inc(s_ptop, 1)
            pe.wait_ge(s_prep, 3)
            pe.matmul(bank[3][:, 0:HEADS + 1], ones[0:HEADS + 1, :], top[0:HEADS + 1, 8:9 + HEADS],
                      start=True, stop=True).then_inc(s_ptop, 1)
            pe.wait_ge(s_prep, PREP_HEAD + 2 * PREP_SIGN)

            def turn_rows(c):
                pe.wait_ge(s_ne, c * NORM_STEPS)
                if not (isinstance(c, int) and c == 1):
                    pe.wait_ge(s_nrow, c - 1)
                for q in range(Q):
                    last = pe.transpose(bank[3][0:SCORES, q * P:(q + 1) * P],
                                        nr[:, q * SCORES:(q + 1) * SCORES], ident[:, :])
                last.then_inc(s_nturn, 1)

            over_chunks(pe, masked("norm", VCOLS, vp, vm, lambda c, g: turn_rows(c) if g == 6 else None))
            turn_sum("norm", C, VCOLS)
            turn_rows(C)

            def spread_rows(c, first_row, banks):
                for k in range(HEADS):
                    r = first_row + k
                    last = pe.matmul(bank[banks[k]][:, :], pick[:, r * P:(r + 1) * P], grows[:, at(c, W, 0, W)],
                                     start=True, stop=True)
                return last

            def gates(c, cell, src):
                h = reg2[:, at(c, W, -W, W)]
                for gate, b in ((0, 5), (1, 6)):
                    pe.matmul(bank[b][:, :], gate_w(cell, 0, gate), src, start=True, stop=False)
                    pe.matmul(bank[b][:, :], gate_w(cell, 1, gate), h, start=False, stop=True)
                pe.matmul(bank[7][:, :], gate_w(cell, 1, 2), h, start=True, stop=True)
                pe.matmul(bank[4][:, :], gate_w(cell, 0, 2), src, start=True, stop=True).then_inc(s_gm, 1)

            def edge_gates(c):
                pe.wait_ge(s_nk, c)
                pe.wait_ge(s_ggk, c + 1)
                pe.wait_ge(s_res, c - 1)
                gates(c, 0, nsT)

            def heads(c):
                pe.wait_ge(s_gv, c * CELL_STEPS + (CELL_A - CELL_STEPS))
                for k in range(HEADS):
                    last = pe.matmul(bank[4][:, :], gat_w[k], nk[:, k * W:(k + 1) * W],
                                     start=(k == 0), stop=(k == HEADS - 1))
                last.then_inc(s_es, 1)

            def spread_dens(c, first):
                if not first:
                    pe.wait_ge(s_gv, c * CELL_STEPS + (CELL_A - CELL_STEPS))
                    pe.wait_ge(s_ga, c * 4 - 3)
                else:
                    pe.wait_ge(s_ggk, 1)
                spread_rows(c, HEADS, (5, 6, 7)).then_inc(s_rr, 1)

            def node_gates(c, last_chunk):
                pe.wait_ge(s_esk, c)
                if not last_chunk:
                    pe.wait_ge(s_rrk, c + 1)
                gates(c, 1, esT)

            def turn_cells(c):
                pe.wait_ge(s_gv, c * CELL_STEPS)
                turn(bank[5], cells).then_inc(s_ot, 1)

            def spread_guards(c, first):
                if not first:
                    pe.wait_ge(s_gv, c * CELL_STEPS + (CELL_B + CELL_A - CELL_STEPS))
                else:
                    pe.wait_ge(s_rrk, 1)
                spread_rows(c + 1, 0, (4, 6, 7)).then_inc(s_gg, 1)

            pe.wait_ge(s_nrow, C)
            spread_rows(0, 0, (4, 6, 7)).then_inc(s_gg, 1)

            def out_body(c, first):
                for g in range(G):
                    for q in range(Q):
                        t = g * Q + q
                        begin, end = t == 0, t == T - 1
                        h = reg1[:, t * P:(t + 1) * P]
                        if begin and not first:
                            pe.wait_ge(s_nk, c)
                        for k in range(HEADS):
                            if k == 0:
                                pe.wait_ge(s_y, c * T + (t + 1))
                            last = pe.matmul(bank[1 + k][:, :], h, tiles(t)[:, k * W:(k + 1) * W],
                                             start=begin, stop=end)
                        last.then_inc(s_used, 1)
                        last = pe.matmul(bank[0][:, :], h, ring[:, ring_at("out", g, q * W, W)],
                                         start=begin, stop=end)
                    last.then_inc(s_mm["out"], 1)
                    if not first:
                        if g == 0:
                            edge_gates(c)
                        if g == 1:
                            heads(c)
                        if g == 3:
                            node_gates(c, False)
                        if g == 5:
                            turn_cells(c)
                    if g == 1:
                        spread_dens(c, first)
                    if g == 6:
                        spread_guards(c, first)
            over_chunks(pe, out_body)
            edge_gates(C)
            heads(C)
            node_gates(C, True)
            turn_cells(C)


def kernel(x, adj, L0_gnn_W, L0_gnn_b, L1_gnn_W, L1_gnn_b, L2_gnn_weight, L2_gnn_a_l, L2_gnn_a_r, L2_gnn_b,
           L3_gnn_gat_W, L3_gnn_gat_a, L3_gnn_edge_Wih, L3_gnn_edge_Whh, L3_gnn_edge_bih, L3_gnn_edge_bhh,
           L3_gnn_node_Wih, L3_gnn_node_Whh, L3_gnn_node_bih, L3_gnn_node_bhh):
    import numpy as np
    import concourse.bacc as bacc
    from concourse.bass_utils import run_bass_kernel_spmd

    x, adj = np.asarray(x), np.asarray(adj)
    gat_w, gat_a = np.asarray(L3_gnn_gat_W), np.asarray(L3_gnn_gat_a)

    def turned(a):
        return np.asarray(a).T

    units = adj.T.reshape(G, Q, P, C, W).transpose(3, 0, 2, 1, 4).reshape(C * G * P, UNIT)
    weights = np.concatenate(
        [turned(L0_gnn_W), turned(L1_gnn_W), np.asarray(L2_gnn_weight), turned(L2_gnn_weight)]
        + [gat_w[k] for k in range(HEADS)] + [gat_w[k].T for k in range(HEADS)], axis=1)
    cells = np.concatenate([turned(w) for w in (L3_gnn_edge_Wih, L3_gnn_edge_Whh, L3_gnn_node_Wih,
                                                L3_gnn_node_Whh)], axis=1)
    columns = np.stack(
        [np.asarray(a) for a in (L1_gnn_b, L2_gnn_a_l, L2_gnn_a_r)]
        + [gat_a[k, h * P:(h + 1) * P, 0] for k in range(HEADS) for h in range(2)]
        + [np.asarray(b)[g * P:(g + 1) * P] for b in (L3_gnn_edge_bih, L3_gnn_edge_bhh, L3_gnn_node_bih,
                                                      L3_gnn_node_bhh) for g in range(3)], axis=1)
    row_pair = np.concatenate([np.asarray(L0_gnn_b), np.asarray(L2_gnn_b)])[None, :]
    arrays = {
        "in_x": x,
        "in_adj_rows": adj,
        "in_adj_units": units,
        "in_adj_diag": np.diagonal(adj).reshape(T, P).T,
        "in_weights": weights,
        "in_cells": cells,
        "in_columns": columns,
        "in_rows": row_pair,
    }
    arrays = {name: np.ascontiguousarray(a) for name, a in arrays.items()}
    nc = bacc.Bacc("TRN2", target_bir_lowering=False, num_devices=1)
    args = [nc.dram_tensor(name, a.shape, F32, kind="ExternalInput").ap() for name, a in arrays.items()]
    out = nc.dram_tensor("out", (N, P), F32, kind="ExternalOutput").ap()
    build(nc, *args, out)
    return run_bass_kernel_spmd(nc, [arrays], core_ids=[0]).results[0]["out"]
```
